# Optimizing a Trainium2 kernel written in Bass

```python
import numpy as np
import jax
import jax.numpy as jnp

def _softmax(x, axis=-1):
    return jax.nn.softmax(x, axis=axis)

def _gelu(x):
    return jax.nn.gelu(x, approximate=True)

def _silu(x):
    return jax.nn.silu(x)

def _sigmoid(x):
    return jax.nn.sigmoid(x)

def _layernorm(x, axis=-1, eps=1e-05):
    m = jnp.mean(x, axis=axis, keepdims=True)
    v = jnp.var(x, axis=axis, keepdims=True)
    return (x - m) / jnp.sqrt(v + eps)

def _scatter_add(tgt, idx, src, axis=0):
    return tgt.at[idx].add(src)

def _segment_sum(src, seg, n):
    return jax.ops.segment_sum(src, seg, n)
kernel_name = 'mk_gps_d1_gnn_r8_05f5f6'

def setup_inputs(seed: int=0):
    np.random.seed(seed)
    _w = jnp.asarray

    def _rec_inputs():
        import jax
        import jax.numpy as jnp
        _gk = jax.random.key(seed)
        x = -0.0003713 + 1 * jax.random.normal(jax.random.fold_in(_gk, 1), (6250, 256), jnp.float32)
        src = jax.random.randint(jax.random.fold_in(_gk, 2), (200000,), 0, 6250, jnp.int32)
        dst = jnp.minimum((6250 * jax.random.uniform(jax.random.fold_in(_gk, 3), (200000,)) ** 2.0).astype(jnp.int32), 49999)
        _o = jnp.argsort(dst, stable=True)
        src = src[_o]
        dst = dst[_o]
        return (x, src, dst)
    x, src, dst = _rec_inputs()

    def _L0_gnn_setup():
        import jax, jax.numpy as jnp
        import numpy as np
        N_NODES = 6250
        N_EDGES = 100000
        IN_FEAT = 256
        HIDDEN = 512
        OUT = 256

        def _sage_conv(x, src, dst, Wl, b, Wr):
            msg_sum = jax.ops.segment_sum(x[src], dst, num_segments=N_NODES)
            deg = jax.ops.segment_sum(jnp.ones((src.shape[0],), x.dtype), dst, num_segments=N_NODES)
            agg = msg_sum / jnp.maximum(deg, 1.0)[:, None]
            return agg @ Wl + b + x @ Wr
        key = jax.random.key(seed)
        ks = jax.random.split(key, 8)
        x = jax.random.normal(ks[0], (N_NODES, IN_FEAT), dtype=jnp.float32)
        edge_index = jax.random.randint(ks[1], (2, N_EDGES), 0, N_NODES, dtype=jnp.int64)
        s1 = 1.0 / np.sqrt(IN_FEAT)
        s2 = 1.0 / np.sqrt(HIDDEN)
        W1l = jax.random.uniform(ks[2], (IN_FEAT, HIDDEN), jnp.float32, -s1, s1)
        b1 = jnp.zeros((HIDDEN,), jnp.float32)
        W1r = jax.random.uniform(ks[3], (IN_FEAT, HIDDEN), jnp.float32, -s1, s1)
        W2l = jax.random.uniform(ks[4], (HIDDEN, OUT), jnp.float32, -s2, s2)
        b2 = jnp.zeros((OUT,), jnp.float32)
        W2r = jax.random.uniform(ks[5], (HIDDEN, OUT), jnp.float32, -s2, s2)
        return {'x': x, 'edge_index': edge_index, 'W1l': W1l, 'b1': b1, 'W1r': W1r, 'W2l': W2l, 'b2': b2, 'W2r': W2r}
    _L0_gnn_all = _L0_gnn_setup()
    _L0_gnn_in = {k: v for k, v in _L0_gnn_all.items() if k in ('W1l', 'b1', 'W1r', 'W2l', 'b2', 'W2r')}
    del _L0_gnn_all

    def _L0_mix_setup():
        import jax, jax.numpy as jnp
        import numpy as np
        C_CURV = 1.0
        MIN_NORM = 1e-15
        BALL_EPS = 1e-05
        ATT_EPS = 1e-15
        DIM = 32

        def _norm(x):
            return jnp.clip(jnp.linalg.norm(x, axis=-1, keepdims=True), MIN_NORM)

        def proj(x, c):
            maxnorm = (1.0 - BALL_EPS) / jnp.sqrt(c)
            n = _norm(x)
            return jnp.where(n > maxnorm, x / n * maxnorm, x)

        def expmap0(u, c):
            sc = jnp.sqrt(c)
            n = _norm(u)
            return jnp.tanh(sc * n) * u / (sc * n)

        def logmap0(p, c):
            sc = jnp.sqrt(c)
            n = _norm(p)
            return jnp.arctanh(jnp.clip(sc * n, -1.0 + 1e-07, 1.0 - 1e-07)) * p / (sc * n)

        def mobius_add(x, y, c):
            x2 = jnp.sum(x * x, -1, keepdims=True)
            y2 = jnp.sum(y * y, -1, keepdims=True)
            xy = jnp.sum(x * y, -1, keepdims=True)
            num = (1 + 2 * c * xy + c * y2) * x + (1 - c * x2) * y
            den = 1 + 2 * c * xy + c * c * x2 * y2
            return num / jnp.clip(den, MIN_NORM)

        def conv1d(x, w, pad, groups=1):
            return jax.lax.conv_general_dilated(x, w, (1,), [(pad, pad)], dimension_numbers=('NCH', 'OIH', 'NCH'), feature_group_count=groups)

        def batchnorm(x, gamma, beta):
            mean = jnp.mean(x, axis=(0, 2), keepdims=True)
            var = jnp.var(x, axis=(0, 2), keepdims=True)
            xn = (x - mean) * jax.lax.rsqrt(var + 1e-05)
            return gamma[None, :, None] * xn + beta[None, :, None]

        def _reference_tuple_inner(x, w_qkv, bn_gamma, bn_beta, w_dw, w_pw, w_res, b_res):
            c = C_CURV
            h = logmap0(proj(x, c), c)
            h = jnp.transpose(h, (1, 2, 0))
            h = conv1d(h, w_qkv, pad=2)
            h = batchnorm(h, bn_gamma, bn_beta)
            h = jax.nn.relu(jnp.transpose(h, (2, 0, 1)))
            qkv = proj(expmap0(h, c), c)
            t = jnp.transpose(logmap0(proj(qkv, c), c), (1, 2, 0))
            s = conv1d(t, w_dw, pad=2, groups=t.shape[1])
            s = conv1d(s, w_pw, pad=0, groups=t.shape[1] // DIM)
            cat = jnp.concatenate([t, s], axis=1)
            ai = proj(expmap0(jnp.transpose(cat, (2, 0, 1)), c), c)
            t2 = logmap0(proj(ai, c), c)
            L, N, C2 = t2.shape
            g = C2 // (3 * DIM)
            qkv3 = jnp.transpose(t2, (1, 2, 0)).reshape(N, g, 3 * DIM, L)
            q, k, v = jnp.split(qkv3, 3, axis=2)
            q = jax.nn.relu(q)
            k = jax.nn.relu(k)
            vk = jnp.einsum('ngdl,ngel->ngde', v, k)
            out = jnp.einsum('ngde,ngdl->ngdl', vk, q)
            out = out / (jnp.sum(v, -1, keepdims=True) + ATT_EPS)
            out = jnp.transpose(out.reshape(N, g * DIM, L), (2, 0, 1))
            fx_h = proj(expmap0(out, c), c)
            ft = jnp.transpose(logmap0(proj(fx_h, c), c), (1, 2, 0))
            ft = conv1d(ft, w_res, pad=0) + b_res[None, :, None]
            fx = proj(expmap0(jnp.transpose(ft, (2, 0, 1)), c), c)
            residual = mobius_add(fx, x, c)
            return (fx, residual)
        key = jax.random.key(seed)
        ks = jax.random.split(key, 6)
        L, N, C, TD = (256, 16, 256, 256)
        x = jax.random.normal(ks[0], (L, N, C), jnp.float32) * 0.05
        w_qkv = jax.random.normal(ks[1], (3 * TD, C, 5), jnp.float32) / np.sqrt(C * 5)
        bn_gamma = jnp.ones((3 * TD,), jnp.float32)
        bn_beta = jnp.zeros((3 * TD,), jnp.float32)
        w_dw = jax.random.normal(ks[2], (3 * TD, 1, 5), jnp.float32) / np.sqrt(5.0)
        w_pw = jax.random.normal(ks[3], (3 * TD, DIM, 1), jnp.float32) / np.sqrt(DIM)
        w_res = jax.random.normal(ks[4], (C, 2 * TD, 1), jnp.float32) / np.sqrt(2 * TD)
        b_res = jnp.zeros((C,), jnp.float32)
        return {'x': x, 'w_qkv': w_qkv, 'bn_gamma': bn_gamma, 'bn_beta': bn_beta, 'w_dw': w_dw, 'w_pw': w_pw, 'w_res': w_res, 'b_res': b_res}
    _L0_mix_all = _L0_mix_setup()
    _L0_mix_in = {k: v for k, v in _L0_mix_all.items() if k in ('w_qkv', 'bn_gamma', 'bn_beta', 'w_dw', 'w_pw', 'w_res', 'b_res')}
    del _L0_mix_all

    def _L0_ffn_setup():
        import jax, jax.numpy as jnp
        import numpy as np
        NUM_EXPERTS = 8
        TOP_K = 2
        B, S, D = (8, 1024, 256)

        def _moe(tokens, router_w, w1, b1, w2, b2):
            N = tokens.shape[0]
            E = router_w.shape[0]
            logits = tokens.astype(jnp.float32) @ router_w.astype(jnp.float32).T
            probs = jax.nn.softmax(logits, axis=-1)
            rw, re = jax.lax.top_k(probs, TOP_K)
            if TOP_K > 1:
                rw = rw / jnp.maximum(rw.sum(-1, keepdims=True), 1e-12)
            rw = rw.astype(tokens.dtype)
            combine = jnp.zeros((N, E), tokens.dtype).at[jnp.arange(N)[:, None], re].set(rw)
            out = tokens
            for e in range(E):
                h = jax.nn.gelu(tokens @ w1[e] + b1[e], approximate=False)
                y = h @ w2[e] + b2[e]
                out = out + combine[:, e:e + 1] * y
            return out
        key = jax.random.key(seed)
        ks = jax.random.split(key, 4)
        scale = 1.0 / np.sqrt(D).astype(np.float32)
        return {'input_embeddings': jax.random.normal(ks[0], (B, S, D), jnp.float32), 'router_w': jax.random.normal(ks[1], (NUM_EXPERTS, D), jnp.float32) * scale, 'w1': jax.random.normal(ks[2], (NUM_EXPERTS, D, D), jnp.float32) * scale, 'b1': jnp.zeros((NUM_EXPERTS, D), jnp.float32), 'w2': jax.random.normal(ks[3], (NUM_EXPERTS, D, D), jnp.float32) * scale, 'b2': jnp.zeros((NUM_EXPERTS, D), jnp.float32)}
    _L0_ffn_all = _L0_ffn_setup()
    _L0_ffn_in = {k: v for k, v in _L0_ffn_all.items() if k in ('router_w', 'w1', 'b1', 'w2', 'b2')}
    del _L0_ffn_all
    return {'x': x, 'src': src, 'dst': dst, 'L0_gnn_W1l': _L0_gnn_in['W1l'], 'L0_gnn_b1': _L0_gnn_in['b1'], 'L0_gnn_W1r': _L0_gnn_in['W1r'], 'L0_gnn_W2l': _L0_gnn_in['W2l'], 'L0_gnn_b2': _L0_gnn_in['b2'], 'L0_gnn_W2r': _L0_gnn_in['W2r'], 'L0_mix_w_qkv': _L0_mix_in['w_qkv'], 'L0_mix_bn_gamma': _L0_mix_in['bn_gamma'], 'L0_mix_bn_beta': _L0_mix_in['bn_beta'], 'L0_mix_w_dw': _L0_mix_in['w_dw'], 'L0_mix_w_pw': _L0_mix_in['w_pw'], 'L0_mix_w_res': _L0_mix_in['w_res'], 'L0_mix_b_res': _L0_mix_in['b_res'], 'L0_ffn_router_w': _L0_ffn_in['router_w'], 'L0_ffn_w1': _L0_ffn_in['w1'], 'L0_ffn_b1': _L0_ffn_in['b1'], 'L0_ffn_w2': _L0_ffn_in['w2'], 'L0_ffn_b2': _L0_ffn_in['b2']}

def reference(x, src, dst, L0_gnn_W1l, L0_gnn_b1, L0_gnn_W1r, L0_gnn_W2l, L0_gnn_b2, L0_gnn_W2r, L0_mix_w_qkv, L0_mix_bn_gamma, L0_mix_bn_beta, L0_mix_w_dw, L0_mix_w_pw, L0_mix_w_res, L0_mix_b_res, L0_ffn_router_w, L0_ffn_w1, L0_ffn_b1, L0_ffn_w2, L0_ffn_b2):
    import jax
    import jax.numpy as jnp

    def _L0_gnn_ref(x, edge_index, W1l, b1, W1r, W2l, b2, W2r):
        import jax, jax.numpy as jnp
        import numpy as np
        N_NODES = 6250
        N_EDGES = 100000
        IN_FEAT = 256
        HIDDEN = 512
        OUT = 256

        def _sage_conv(x, src, dst, Wl, b, Wr):
            msg_sum = jax.ops.segment_sum(x[src], dst, num_segments=N_NODES)
            deg = jax.ops.segment_sum(jnp.ones((src.shape[0],), x.dtype), dst, num_segments=N_NODES)
            agg = msg_sum / jnp.maximum(deg, 1.0)[:, None]
            return agg @ Wl + b + x @ Wr
        src, dst = (edge_index[0], edge_index[1])
        h = jax.nn.relu(_sage_conv(x, src, dst, W1l, b1, W1r))
        return _sage_conv(h, src, dst, W2l, b2, W2r)

    def _L0_mix_ref(x, w_qkv, bn_gamma, bn_beta, w_dw, w_pw, w_res, b_res):
        import jax, jax.numpy as jnp
        import numpy as np
        C_CURV = 1.0
        MIN_NORM = 1e-15
        BALL_EPS = 1e-05
        ATT_EPS = 1e-15
        DIM = 32

        def _norm(x):
            return jnp.clip(jnp.linalg.norm(x, axis=-1, keepdims=True), MIN_NORM)

        def proj(x, c):
            maxnorm = (1.0 - BALL_EPS) / jnp.sqrt(c)
            n = _norm(x)
            return jnp.where(n > maxnorm, x / n * maxnorm, x)

        def expmap0(u, c):
            sc = jnp.sqrt(c)
            n = _norm(u)
            return jnp.tanh(sc * n) * u / (sc * n)

        def logmap0(p, c):
            sc = jnp.sqrt(c)
            n = _norm(p)
            return jnp.arctanh(jnp.clip(sc * n, -1.0 + 1e-07, 1.0 - 1e-07)) * p / (sc * n)

        def mobius_add(x, y, c):
            x2 = jnp.sum(x * x, -1, keepdims=True)
            y2 = jnp.sum(y * y, -1, keepdims=True)
            xy = jnp.sum(x * y, -1, keepdims=True)
            num = (1 + 2 * c * xy + c * y2) * x + (1 - c * x2) * y
            den = 1 + 2 * c * xy + c * c * x2 * y2
            return num / jnp.clip(den, MIN_NORM)

        def conv1d(x, w, pad, groups=1):
            return jax.lax.conv_general_dilated(x, w, (1,), [(pad, pad)], dimension_numbers=('NCH', 'OIH', 'NCH'), feature_group_count=groups)

        def batchnorm(x, gamma, beta):
            mean = jnp.mean(x, axis=(0, 2), keepdims=True)
            var = jnp.var(x, axis=(0, 2), keepdims=True)
            xn = (x - mean) * jax.lax.rsqrt(var + 1e-05)
            return gamma[None, :, None] * xn + beta[None, :, None]

        def _reference_tuple_inner(x, w_qkv, bn_gamma, bn_beta, w_dw, w_pw, w_res, b_res):
            c = C_CURV
            h = logmap0(proj(x, c), c)
            h = jnp.transpose(h, (1, 2, 0))
            h = conv1d(h, w_qkv, pad=2)
            h = batchnorm(h, bn_gamma, bn_beta)
            h = jax.nn.relu(jnp.transpose(h, (2, 0, 1)))
            qkv = proj(expmap0(h, c), c)
            t = jnp.transpose(logmap0(proj(qkv, c), c), (1, 2, 0))
            s = conv1d(t, w_dw, pad=2, groups=t.shape[1])
            s = conv1d(s, w_pw, pad=0, groups=t.shape[1] // DIM)
            cat = jnp.concatenate([t, s], axis=1)
            ai = proj(expmap0(jnp.transpose(cat, (2, 0, 1)), c), c)
            t2 = logmap0(proj(ai, c), c)
            L, N, C2 = t2.shape
            g = C2 // (3 * DIM)
            qkv3 = jnp.transpose(t2, (1, 2, 0)).reshape(N, g, 3 * DIM, L)
            q, k, v = jnp.split(qkv3, 3, axis=2)
            q = jax.nn.relu(q)
            k = jax.nn.relu(k)
            vk = jnp.einsum('ngdl,ngel->ngde', v, k)
            out = jnp.einsum('ngde,ngdl->ngdl', vk, q)
            out = out / (jnp.sum(v, -1, keepdims=True) + ATT_EPS)
            out = jnp.transpose(out.reshape(N, g * DIM, L), (2, 0, 1))
            fx_h = proj(expmap0(out, c), c)
            ft = jnp.transpose(logmap0(proj(fx_h, c), c), (1, 2, 0))
            ft = conv1d(ft, w_res, pad=0) + b_res[None, :, None]
            fx = proj(expmap0(jnp.transpose(ft, (2, 0, 1)), c), c)
            residual = mobius_add(fx, x, c)
            return (fx, residual)
        return _reference_tuple_inner(x, w_qkv, bn_gamma, bn_beta, w_dw, w_pw, w_res, b_res)[0]

    def _L0_ffn_ref(input_embeddings, router_w, w1, b1, w2, b2):
        import jax, jax.numpy as jnp
        import numpy as np
        NUM_EXPERTS = 8
        TOP_K = 2
        B, S, D = (8, 1024, 256)

        def _moe(tokens, router_w, w1, b1, w2, b2):
            N = tokens.shape[0]
            E = router_w.shape[0]
            logits = tokens.astype(jnp.float32) @ router_w.astype(jnp.float32).T
            probs = jax.nn.softmax(logits, axis=-1)
            rw, re = jax.lax.top_k(probs, TOP_K)
            if TOP_K > 1:
                rw = rw / jnp.maximum(rw.sum(-1, keepdims=True), 1e-12)
            rw = rw.astype(tokens.dtype)
            combine = jnp.zeros((N, E), tokens.dtype).at[jnp.arange(N)[:, None], re].set(rw)
            out = tokens
            for e in range(E):
                h = jax.nn.gelu(tokens @ w1[e] + b1[e], approximate=False)
                y = h @ w2[e] + b2[e]
                out = out + combine[:, e:e + 1] * y
            return out
        b, s, d = input_embeddings.shape
        tokens = input_embeddings.reshape(b * s, d)
        return _moe(tokens, router_w, w1, b1, w2, b2).reshape(b, s, d)
    edge_index = jnp.stack([src, dst])
    xn = _layernorm(x, axis=-1)
    x = x + _L0_gnn_ref(xn, edge_index, L0_gnn_W1l, L0_gnn_b1, L0_gnn_W1r, L0_gnn_W2l, L0_gnn_b2, L0_gnn_W2r) + _L0_mix_ref(xn[None], L0_mix_w_qkv, L0_mix_bn_gamma, L0_mix_bn_beta, L0_mix_w_dw, L0_mix_w_pw, L0_mix_w_res, L0_mix_b_res)[0]
    x = x + _L0_ffn_ref(_layernorm(x, axis=-1)[None], L0_ffn_router_w, L0_ffn_w1, L0_ffn_b1, L0_ffn_w2, L0_ffn_b2)[0]
    return x

_drawn_inputs = setup_inputs


def setup_inputs(seed=0):
    import zlib

    import numpy as np

    out = dict(_drawn_inputs(seed))
    spreads = {'L0_gnn_b1': (0.0, 0.1),
     'L0_gnn_b2': (0.0, 0.1),
     'L0_mix_bn_gamma': (1.0, 0.6),
     'L0_mix_bn_beta': (0.0, 0.85),
     'L0_mix_b_res': (0.0, 0.1),
     'L0_ffn_b1': (0.0, 0.33),
     'L0_ffn_b2': (0.0, 0.1)}
    factors = {'L0_mix_w_dw': 3.794, 'L0_mix_w_pw': 3.848}
    for name, (base, spread) in spreads.items():
        noise = np.random.default_rng([zlib.crc32(name.encode()), seed]).standard_normal(out[name].shape)
        drawn = base * np.exp(spread * noise) if base else spread * noise
        out[name] = jnp.asarray(drawn.astype(out[name].dtype))
    for name, factor in factors.items():
        out[name] = (out[name] * factor).astype(out[name].dtype)
    return out
```

```python
from contextlib import ExitStack

import concourse.bass as bass
from concourse import mybir

F32 = mybir.dt.float32
I32 = mybir.dt.int32
ALU = mybir.AluOpType
ACT = mybir.ActivationFunctionType
AX = mybir.AxisListType
P = 128

N = 6250
E = 200000
D = 256
HID = 512
CH = 768
NT = -(-N // P)
NPAIR = (NT + 1) // 2
NT2 = 2 * NPAIR
NROWS = NT2 * P
LAST = N - (NT - 1) * P
ET = -(-E // P)
RING = 16
BANK = RING // 2
ITER = -(-(ET + NT - 1) // RING)
ITEMS = ITER * RING
IC = -(-ITEMS // P)
IPAD = IC * P
NE = 8
ACCW = D + 1

MAXNORM = 1.0 - 1e-5
ATANH_MAX = 6.1030339
LOG_EPS = 1e-15
LN_EPS = 1e-5


class Buffers:
    pass


class Sems:

    def __init__(self, ctx, nc, prefix):
        self.ctx, self.nc, self.prefix = ctx, nc, prefix

    def __call__(self, name):
        return self.ctx.enter_context(self.nc.semaphore(f"{self.prefix}_{name}"))


class Chain:

    def __init__(self, eng, sem):
        self.eng, self.sem, self.n = eng, sem, 0

    def restart(self):
        self.eng.sem_clear(self.sem)
        self.n = 0

    def do(self, ins):
        self.n += 1
        ins.then_inc(self.sem, 1)
        self.eng.wait_ge(self.sem, self.n)


class Step:

    def __init__(self, sem, ring, per=1):
        self.sem, self.ring, self.per = sem, ring, per

    def start(self, eng):
        eng.sem_inc(self.sem, self.ring)

    def done(self, ins):
        ins.then_inc(self.sem, 1)

    def after(self, eng, p, c=0):
        eng.wait_ge(self.sem, p * self.per + (c + 1 + self.ring))

    def free(self, eng, p, c=0):
        eng.wait_ge(self.sem, p * self.per + (c + 1))


def pairs(ap, p):
    return ap[bass.ds(p * 2 * P, 2 * P), :].rearrange("(j q) f -> q j f", q=P)


def flat(ap):
    return ap.rearrange("p a w -> p (a w)")


def over_pairs(eng, body):
    with eng.Fori(0, NPAIR // 2) as i:
        body(i * 2, i, 0)
        body(i * 2 + 1, i, 1)
    body(NPAIR - 1, NPAIR // 2, 0)


def over_pairs_ahead(eng, front, main):
    front(0, 0, 0)
    with eng.Fori(0, NPAIR // 2) as i:
        front(i * 2 + 1, i, 1)
        main(i * 2, i, 0)
        front(i * 2 + 2, i + 1, 0)
        main(i * 2 + 1, i, 1)
    main(NPAIR - 1, NPAIR // 2, 0)


def gnn_mix_moe(nc, a, out):
    top = ExitStack()
    b = Buffers()
    with top:
        def sbuf(ctx, name, shape, dt=F32):
            return ctx.enter_context(nc.sbuf_tensor(name, shape, dt))

        def psum(ctx, name, shape):
            return ctx.enter_context(nc.psum_tensor(name, shape, F32))

        def scratch(name, shape, dt=F32):
            return nc.dram_tensor(name, shape, dt, kind="Internal").ap()

        b.xp_d = scratch("xp_d", (NROWS, D))
        b.xn_d = scratch("xn_d", (NROWS, D))
        b.y_d = scratch("y_d", (NROWS, D))
        b.z_d = scratch("z_d", (NROWS, D))
        b.ft_d = scratch("ft_d", (NROWS, D))
        b.srcp_d = scratch("srcp_d", (IPAD, P), I32)
        b.dstp_d = scratch("dstp_d", (IPAD, P), I32)
        b.blk_d = scratch("blk_d", (IC, P), I32)

        b.X = sbuf(top, "X", [P, NT2, D])
        b.acc = sbuf(top, "acc", [P, NT2, ACCW])
        b.ident = sbuf(top, "ident", [P, P])
        b.scale_h = sbuf(top, "scale_h", [P, NT2])
        b.ft_sq = sbuf(top, "ft_sq", [P, NT2])
        b.b2_bc = sbuf(top, "b2_bc", [P, D])
        b.bres_bc = sbuf(top, "bres_bc", [P, D])
        b.moe_b1 = sbuf(top, "moe_b1", [P, NE, 2])
        b.moe_b2 = sbuf(top, "moe_b2", [NE, D])
        b.router = sbuf(top, "router", [P, 2, NE])
        b.rdeg = sbuf(top, "rdeg", [P, NT2])
        b.sorted_f = sbuf(top, "sorted_f", [P, 1])
        b.unsorted_i = sbuf(top, "unsorted_i", [1, 1], I32)

        early = ExitStack()
        b.srcT = sbuf(early, "srcT", [P, IPAD], I32)
        b.dstT = sbuf(early, "dstT", [P, IPAD])
        b.blk_row = sbuf(early, "blk_row", [1, IPAD], I32)
        b.iota = sbuf(early, "iota", [P, P])
        b.rows = sbuf(early, "rows", [P, RING, ACCW])
        b.onehot = sbuf(early, "onehot", [P, 4, P])
        b.ix = sbuf(early, "ix", [P, RING], I32)
        b.b1 = sbuf(early, "b1", [P, 4])
        b.bn_a = sbuf(early, "bn_a", [P, 6])
        b.bn_b = sbuf(early, "bn_b", [P, 6])

        setup(nc, a, b)
        mix = ExitStack()
        b.wq = sbuf(mix, "wq", [P, 2, CH])
        b.pw = sbuf(mix, "pw", [P, 6, P])
        b.wres = sbuf(mix, "wres", [P, 4, D])
        mixing_stats(nc, a, b)
        aggregate(nc, "g1", b.xn_d, b, with_degree=True)
        mixing(nc, a, b)
        mix.close()
        sage_dense(nc, a, b)
        aggregate(nc, "g2", b.y_d, b, with_degree=False)
        early.close()
        finish(nc, a, b, out)


def setup(nc, a, b):
    X, xn_d, ident, iota = b.X, b.xn_d, b.ident, b.iota
    srcp_d, dstp_d, blk_d = b.srcp_d, b.dstp_d, b.blk_d
    srcT, dstT, blk_row, rows, scale_h = b.srcT, b.dstT, b.blk_row, b.rows, b.scale_h
    sorted_f, unsorted_i = b.sorted_f, b.unsorted_i
    PADE = IPAD * P - E
    PR = 116
    assert PADE % PR == 0
    CHK = 100
    CL = E // CHK
    with ExitStack() as ctx:
        used = [0]

        def sb(name, shape, dt=F32):
            words = shape[1] * (shape[2] if len(shape) == 3 else 1)
            t = acc[0:shape[0], used[0]:used[0] + words]
            used[0] += words
            if dt is not F32:
                t = t.bitcast(dt)
            return t.rearrange("p (a w) -> p a w", w=shape[2]) if len(shape) == 3 else t

        acc = b.acc[:, :, :].rearrange("p t w -> p (t w)")
        sem = Sems(ctx, nc, "su")
        fill0 = sb("fill0", [PR, PADE // PR], I32)
        fillm = sb("fillm", [PR, PADE // PR], I32)
        zrow = sb("zrow", [50, (NROWS - N) // 50 * D])
        chk = sb("chk", [CHK, CL + 1], I32)
        viol = sb("viol", [CHK, 1])
        ones = sb("ones", [P, P])
        last_i = sb("last_i", [1, ET], I32)
        key = last_i.bitcast(F32)
        tix = sb("tix", [1, ET])
        item_f = sb("item_f", [P, IC])
        tile_f = sb("tile_f", [P, IC])
        tile_i = sb("tile_i", [P, IC], I32)
        blk_f = sb("blk_f", [P, IC])
        blk_i = sb("blk_i", [P, IC], I32)
        junk = sb("junk", [P, CL])
        itS = sb("itS", [P, IC, P], I32)
        itD = sb("itD", [P, IC, P], I32)
        stats = sb("stats", [P, NT2, 6])
        mv = sb("mv", [P, NT2, 2])
        rstd = sb("rstd", [P, NT2])
        nrm = sb("nrm", [P, NT2])
        t1 = sb("t1", [P, NT2])
        t2 = sb("t2", [P, NT2])
        t3 = sb("t3", [P, NT2])
        sq_out = sb("sq_out", [P, D])
        itSf = itS[:, :, :].bitcast(F32)
        itDf = itD[:, :, :].bitcast(F32)

        key_ps = ctx.enter_context(nc.psum_tensor("key_ps", [P, 2048], F32))
        tr_ps = ctx.enter_context(nc.psum_tensor("tr_ps", [P, 2, 512], F32))
        sum_ps = ctx.enter_context(nc.psum_tensor("sum_ps", [P, 8], F32))

        xp_out = sem("xp_out")
        fills, padded, x_in, last_in, chk_in = sem("fills"), sem("padded"), sem("x_in"), sem("last_in"), sem("chk_in")
        weights_in, consts, chk_set = sem("weights_in"), sem("consts"), sem("chk_set")
        viol_ready, viol_sum, key_ready, key_bc = sem("viol_ready"), sem("viol_sum"), sem("key_ready"), sem("key_bc")
        tiles_ready, blk_ready, blk_out, items_in = sem("tiles_ready"), sem("blk_ready"), sem("blk_out"), sem("items_in")
        tabs_ready, tr_done, tr_used, blk_back = sem("tabs_ready"), sem("tr_done"), sem("tr_used"), sem("blk_back")
        var_ready, std_ready, xn_ready, sq_ready, nrm_ready = (sem("var_ready"), sem("std_ready"), sem("xn_ready"),
                                                              sem("sq_ready"), sem("nrm_ready"))
        lnin_ready, ln_ready, xn_out, zeroed = sem("lnin_ready"), sem("ln_ready"), sem("xn_out"), sem("zeroed")
        chain_v, chain_p, chain_a = sem("chain_v"), sem("chain_p"), sem("chain_a")
        block = ctx.enter_context(nc.Block())

        @block.sync
        def _(sp):
            with nc.allow_non_contiguous_dma(reason="last edge of each tile; small tables"):
                sp.wait_ge(zeroed, 1)
                sp.dma_start(X[:, 0:NT - 1, :], a["x"][0:(NT - 1) * P, :].rearrange("(t p) f -> p t f", p=P)
                             ).then_inc(x_in, 16)
                sp.dma_start(X[0:LAST, NT - 1, :], a["x"][(NT - 1) * P:N, :]).then_inc(x_in, 16)
                sp.dma_start(b.xp_d[0:N, :].rearrange("(q r) f -> q (r f)", q=50), a["x"].rearrange("(q r) f -> q (r f)", q=50)
                             ).then_inc(xp_out, 16)
                sp.wait_ge(fills, 3)
                sp.dma_start(b.xp_d[N:NROWS, :].rearrange("(q r) f -> q (r f)", q=50), zrow[:, :]).then_inc(xp_out, 16)
                sp.dma_start(last_i[0:1, 0:ET - 1], a["dst"][0:(ET - 1) * P].rearrange("(o t p) -> o t p", o=1, p=P)[:, :, P - 1]
                             ).then_inc(last_in, 16)
                sp.dma_start(last_i[0:1, ET - 1:ET], a["dst"][E - 1:E].rearrange("(o t) -> o t", o=1)).then_inc(last_in, 16)
                sp.wait_ge(chk_set, 1)
                sp.dma_start(chk[:, 0:CL], a["dst"].rearrange("(p c) -> p c", p=CHK)).then_inc(chk_in, 16)
                sp.dma_start(chk[0:CHK - 1, CL:CL + 1], a["dst"][CL:E].rearrange("(p c) -> p c", c=CL)[:, 0:1]
                             ).then_inc(chk_in, 16)
                for d, s, f in ((srcp_d, a["src"], fill0), (dstp_d, a["dst"], fillm)):
                    flat = d.rearrange("t p -> (t p)")
                    sp.dma_start(flat[0:E].rearrange("(q n) -> q n", q=16), s.rearrange("(q n) -> q n", q=16)
                                 ).then_inc(padded, 16)
                    sp.wait_ge(fills, 2)
                    sp.dma_start(flat[E:IPAD * P].rearrange("(q n) -> q n", q=PR), f[:, :]).then_inc(padded, 16)
                loads = [
                    (b.b1[:, :], a["b1"].rearrange("(k p) -> p k", p=P)),
                    (b.b2_bc[:, :], a["b2"].rearrange("(o n) -> o n", o=1).to_broadcast([P, D])),
                    (b.bres_bc[:, :], a["b_res"].rearrange("(o n) -> o n", o=1).to_broadcast([P, D])),
                    (b.router[:, :, :], a["routerT"].rearrange("(k p) e -> p k e", p=P)),
                    (b.moe_b1[:, :, :], a["eb1"].rearrange("e (m p) -> p e m", p=P)),
                    (b.moe_b2[:, :], a["eb2"]),
                    (b.bn_a[:, :], a["gamma"].rearrange("(m p) -> p m", p=P)),
                    (b.bn_b[:, :], a["beta"].rearrange("(m p) -> p m", p=P)),
                ]
                for dst, src in loads:
                    sp.dma_start(dst, src).then_inc(weights_in, 16)
                sp.wait_ge(blk_ready, 1)
                sp.dma_start(blk_d.rearrange("c p -> p c"), blk_i[:, :]).then_inc(blk_out, 16)
                sp.wait_ge(blk_out, 16)
                sp.dma_start(blk_row[0:1, :], blk_d.rearrange("c p -> (c p)").rearrange("(o n) -> o n", o=1)
                             ).then_inc(blk_back, 16)
                sp.wait_ge(xn_ready, 1)
                sp.dma_start(xn_d.rearrange("(t p) f -> p t f", p=P), X[:, :, :]).then_inc(xn_out, 16)
                sp.wait_ge(xn_out, 16)
                sp.wait_ge(xp_out, 32)
                sp.wait_ge(blk_back, 16)
                sp.wait_ge(weights_in, 16 * len(loads))

        @block.gpsimd
        def _(pool):
            ch = Chain(pool, chain_p)
            pool.memset(fill0[:, :], 0).then_inc(fills, 1)
            pool.memset(fillm[:, :], -1).then_inc(fills, 1)
            pool.memset(zrow[:, :], 0.0).then_inc(fills, 1)
            pool.memset(chk[:, :], 1 << 23).then_inc(chk_set, 1)
            ch.do(pool.memset(ident[:, :], 0.0))
            ch.do(pool.affine_select(out=ident[:, :], in_=ident[:, :], compare_op=ALU.not_equal, fill=1.0, base=0,
                                     pattern=[[-1, P]], channel_multiplier=1))
            pool.iota(iota[:, :], pattern=[[1, P]], base=0, channel_multiplier=0, allow_small_or_imprecise_dtypes=True
                      ).then_inc(consts, 1)
            pool.iota(tix[:, :], pattern=[[1, ET]], base=0, channel_multiplier=0, allow_small_or_imprecise_dtypes=True
                      ).then_inc(consts, 1)
            pool.iota(item_f[:, :], pattern=[[P, IC]], base=0, channel_multiplier=1, allow_small_or_imprecise_dtypes=True
                      ).then_inc(consts, 1)
            pool.memset(ones[:, :], 1.0).then_inc(consts, 1)
            pool.memset(rows[:, :, D:D + 1], 1.0).then_inc(consts, 1)
            pool.wait_ge(tiles_ready, 1)
            pool.wait_ge(padded, 64)
            for table, d in ((itS, srcp_d), (itD, dstp_d)):
                for c in range(IC):
                    pool.indirect_dma_start(table[:, c, :], None, d[:, :],
                                            bass.IndirectOffsetOnAxis(ap=tile_i[:, c:c + 1], axis=0)
                                            ).then_inc(items_in, 16)

        @block.vector
        def _(dve):
            ch = Chain(dve, chain_v)
            nc.vector.memset(X[:, NT - 1:NT2, :], 0.0).then_inc(zeroed, 1)
            dve.wait_ge(chk_in, 32)
            ch.do(nc.vector.tensor_tensor(junk[0:CHK, :], chk[:, 0:CL], chk[:, 1:CL + 1], ALU.is_gt))
            nc.vector.tensor_reduce(out=viol[:, :], in_=junk[0:CHK, :], op=ALU.add, axis=AX.X).then_inc(viol_ready, 1)
            dve.wait_ge(viol_sum, 1)
            nc.vector.tensor_scalar(unsorted_i[0:1, 0:1], sum_ps[0:1, 0:1], 0.5, None, ALU.is_gt)
            ch.do(nc.vector.tensor_scalar(sorted_f[:, :], sum_ps[:, 0:1], 0.5, None, ALU.is_lt))
            dve.wait_ge(last_in, 32)
            dve.wait_ge(consts, 5)
            ch.do(nc.vector.tensor_scalar(last_i[:, :], last_i[:, :], 0.0, float(NT * P - 1), ALU.max, ALU.min))
            ch.do(nc.vector.tensor_scalar(last_i[:, :], last_i[:, :], 7, None, ALU.arith_shift_right))
            nc.vector.scalar_tensor_tensor(out=key[:, :], in0=last_i[:, :], scalar=sorted_f[0:1, 0:1], in1=tix[:, :],
                                           op0=ALU.mult, op1=ALU.add).then_inc(key_ready, 1)
            dve.wait_ge(key_bc, 1)
            for c in range(IC):
                ch.do(nc.vector.tensor_scalar(junk[:, 0:ET], key_ps[:, 0:ET], item_f[:, c:c + 1], None, ALU.is_lt,
                                              ALU.add, accum_out=tile_f[:, c:c + 1]))
            nc.vector.tensor_copy(tile_i[:, :], tile_f[:, :]).then_inc(tiles_ready, 1)
            ch.do(nc.vector.tensor_tensor(blk_f[:, :], item_f[:, :], tile_f[:, :], ALU.subtract))
            ch.do(nc.vector.tensor_scalar(blk_f[:, :], blk_f[:, :], float(NT - 1), sorted_f[:, 0:1], ALU.min, ALU.mult))
            ch.do(nc.vector.tensor_copy(blk_i[:, :], blk_f[:, :]))
            dve.sem_inc(blk_ready, 1)
            ch.do(nc.vector.tensor_scalar(blk_f[:, :], blk_f[:, :], float(P), None, ALU.mult))
            dve.wait_ge(x_in, 32)
            for t in range(NT2):
                last = nc.vector.bn_stats(stats[:, t, :], X[:, t, :])
            ch.do(last)
            for t in range(NT2):
                last = nc.vector.bn_aggr(mv[:, t, :], stats[:, t, :])
            ch.do(last)
            nc.vector.tensor_scalar(rstd[:, :], mv[:, :, 1], LN_EPS, None, ALU.add).then_inc(var_ready, 1)
            dve.wait_ge(std_ready, 1)
            ch.do(nc.vector.reciprocal(rstd[:, :], rstd[:, :]))
            for t in range(NT2):
                last = nc.vector.tensor_scalar(X[:, t, :], X[:, t, :], mv[:, t, 0:1], rstd[:, t:t + 1],
                                               ALU.subtract, ALU.mult)
            last.then_inc(xn_ready, 1)
            dve.wait_ge(items_in, 16 * 2 * IC)
            for c in range(IC):
                nc.vector.tensor_scalar(itDf[:, c, :], itD[:, c, :], blk_f[:, c:c + 1], None, ALU.subtract)
                last = nc.vector.tensor_copy(itSf[:, c, :], itS[:, c, :])
            last.then_inc(tabs_ready, 1)
            for c in range(IC):
                dve.wait_ge(tr_done, c + 1)
                nc.vector.tensor_copy(srcT[:, c * P:(c + 1) * P], tr_ps[:, c % 2, 0:P])
                nc.vector.tensor_copy(dstT[:, c * P:(c + 1) * P], tr_ps[:, c % 2, P:2 * P]).then_inc(tr_used, 1)
            dve.wait_ge(nrm_ready, 1)
            ch.do(nc.vector.tensor_scalar(t1[:, :], nrm[:, :], MAXNORM, None, ALU.min))
            ch.do(nc.vector.tensor_scalar(t2[:, :], t1[:, :], 1.0, None, ALU.add))
            ch.do(nc.vector.tensor_scalar(t3[:, :], t1[:, :], -1.0, 1.0, ALU.mult, ALU.add))
            ch.do(nc.vector.reciprocal(t3[:, :], t3[:, :]))
            nc.vector.tensor_tensor(t2[:, :], t2[:, :], t3[:, :], ALU.mult).then_inc(lnin_ready, 1)
            dve.wait_ge(ln_ready, 1)
            ch.do(nc.vector.tensor_scalar(nrm[:, :], nrm[:, :], LOG_EPS, None, ALU.max))
            ch.do(nc.vector.reciprocal(t3[:, :], nrm[:, :]))
            ch.do(nc.vector.scalar_tensor_tensor(out=scale_h[:, :], in0=t2[:, :], scalar=0.5, in1=t3[:, :],
                                                 op0=ALU.mult, op1=ALU.mult))
            ch.do(nc.vector.tensor_scalar(nrm[:, :], t1[:, :], 0.1, None, ALU.is_lt))
            ch.do(nc.vector.tensor_tensor(t2[:, :], t1[:, :], t1[:, :], ALU.mult))
            ch.do(nc.vector.tensor_tensor(t3[:, :], t1[:, :], t3[:, :], ALU.mult))
            ch.do(nc.vector.tensor_scalar(t1[:, :], t2[:, :], 1.0 / 7, 1.0 / 5, ALU.mult, ALU.add))
            ch.do(nc.vector.tensor_tensor(t1[:, :], t1[:, :], t2[:, :], ALU.mult))
            ch.do(nc.vector.tensor_scalar(t1[:, :], t1[:, :], 1.0 / 3, None, ALU.add))
            ch.do(nc.vector.tensor_tensor(t1[:, :], t1[:, :], t2[:, :], ALU.mult))
            ch.do(nc.vector.tensor_scalar(t1[:, :], t1[:, :], 1.0, None, ALU.add))
            ch.do(nc.vector.tensor_tensor(t1[:, :], t1[:, :], t3[:, :], ALU.mult))
            ch.do(nc.vector.tensor_tensor(t1[:, :], t1[:, :], scale_h[:, :], ALU.subtract))
            ch.do(nc.vector.tensor_tensor(t1[:, :], t1[:, :], nrm[:, :], ALU.mult))
            ch.do(nc.vector.tensor_tensor(scale_h[:, :], scale_h[:, :], t1[:, :], ALU.add))

        @block.scalar
        def _(act):
            act.wait_ge(var_ready, 1)
            nc.scalar.activation(rstd[:, :], rstd[:, :], ACT.Sqrt).then_inc(std_ready, 1)
            act.wait_ge(xn_ready, 1)
            ch = Chain(act, chain_a)
            for t in range(NT2):
                ch.do(nc.scalar.activation(sq_out[:, :], X[:, t, :], ACT.Square, accum_out=nrm[:, t:t + 1]))
            nc.scalar.activation(nrm[:, :], nrm[:, :], ACT.Sqrt).then_inc(nrm_ready, 1)
            act.wait_ge(lnin_ready, 1)
            nc.scalar.activation(t2[:, :], t2[:, :], ACT.Ln).then_inc(ln_ready, 1)

        @block.tensor
        def _(pe):
            pe.wait_ge(consts, 5)
            pe.wait_ge(viol_ready, 1)
            nc.tensor.matmul(sum_ps[:, 0:1], ones[0:CHK, :], viol[:, :], start=True, stop=True).then_inc(viol_sum, 1)
            pe.wait_ge(key_ready, 1)
            for c in range(0, ET, 512):
                n = min(512, ET - c)
                last = nc.tensor.matmul(key_ps[:, c:c + n], ones[0:1, :], key[0:1, c:c + n], start=True, stop=True)
            last.then_inc(key_bc, 1)
            pe.wait_ge(tabs_ready, 1)
            for c in range(IC):
                if c >= 2:
                    pe.wait_ge(tr_used, c - 1)
                nc.tensor.transpose(tr_ps[:, c % 2, 0:P], itSf[:, c, :], ident[:, :])
                nc.tensor.transpose(tr_ps[:, c % 2, P:2 * P], itDf[:, c, :], ident[:, :]).then_inc(tr_done, 1)


def aggregate(nc, name, table_d, b, with_degree):
    acc, rows, onehot, ix = b.acc, b.rows, b.onehot, b.ix
    srcT, dstT, blk_row, iota, unsorted_i = b.srcT, b.dstT, b.blk_row, b.iota, b.unsorted_i
    W = ACCW if with_degree else D
    with ExitStack() as ctx:
        sem = Sems(ctx, nc, name)
        ps = ctx.enter_context(nc.psum_tensor(f"{name}_ps", [P, 2, 512], F32))
        gathered = [sem(f"gathered{k}") for k in range(RING)]
        bank_ready = [sem(f"bank_ready{bank}") for bank in range(2)]
        onehot_ready, item_done, added, zeroed, shifted = (sem("onehot_ready"), sem("item_done"), sem("added"),
                                                          sem("zeroed"), sem("shifted"))
        block = ctx.enter_context(nc.Block())

        def rounds(eng, body, between=None):
            with eng.Fori(0, ITER) as it:
                body(it, 0, it, further=False)
            flag = eng.value_load(unsorted_i[0:1, 0:1], min_val=0, max_val=1)
            with eng.If(flag > 0):
                with eng.Fori(1, NT) as r:
                    if between:
                        between(r)
                    with eng.Fori(0, ITER) as it:
                        body(it, r, r * ITER + it)

        @block.gpsimd
        def _(pool):
            def body(it, r, n, further=True):
                for bank in range(2):
                    pool.wait_ge(bank_ready[bank], 1)
                    pool.sem_clear(bank_ready[bank])
                    for k in range(bank * BANK, (bank + 1) * BANK):
                        pool.indirect_dma_start(rows[:, k, 0:D], None, table_d[:, :],
                                                bass.IndirectOffsetOnAxis(ap=ix[:, k:k + 1], axis=0)
                                                ).then_inc(gathered[k], 16)
            rounds(pool, body)

        @block.scalar
        def _(act):
            def body(it, r, n, further=True):
                for bank in range(2):
                    act.wait_ge(item_done, n * RING + (bank + 1) * BANK)
                    nc.scalar.copy(ix[:, bank * BANK:(bank + 1) * BANK], srcT[:, bass.ds(it * RING + bank * BANK, BANK)]
                                   ).then_inc(bank_ready[bank], 1)
            rounds(act, body)

        @block.vector
        def _(dve):
            nc.vector.memset(acc[:, :, 0:W], 0.0).then_inc(zeroed, 1)
            dve.wait_ge(zeroed, 1)
            dve.sem_inc(added, 2)

            def body(it, r, n, further=True):
                def make_onehot(k):
                    dve.wait_ge(item_done, n * RING + k + 1 + RING - 4)
                    nc.vector.tensor_scalar(onehot[:, k % 4, :], iota[:, :], dstT[:, bass.ds(it * RING + k, 1)],
                                            None, ALU.is_equal).then_inc(onehot_ready, 1)

                def add(k):
                    blk = r if further else dve.value_load(blk_row[0:1, bass.ds(it * RING + k, 1)],
                                                           min_val=0, max_val=NT - 1)
                    at = acc[:, bass.ds(blk, 1), 0:W].rearrange("p o w -> p (o w)")
                    dve.wait_ge(item_done, n * RING + k + 1 + RING)
                    dve.wait_ge(added, n * RING + k + 2)
                    nc.vector.tensor_tensor(at, at, ps[:, k % 2, 0:W], ALU.add).then_inc(added, 1)

                for k in range(RING + 2):
                    if k < RING:
                        make_onehot(k)
                    if k >= 2:
                        add(k - 2)

            ch = Chain(dve, shifted)

            def between(r):
                ch.restart()
                ch.do(nc.vector.tensor_scalar(dstT[:, :], dstT[:, :], float(P), None, ALU.subtract))
            rounds(dve, body, between)
            flag = dve.value_load(unsorted_i[0:1, 0:1], min_val=0, max_val=1)
            with dve.If(flag > 0):
                ch.restart()
                ch.do(nc.vector.tensor_scalar(dstT[:, :], dstT[:, :], float(P * (NT - 1)), None, ALU.add))

        @block.tensor
        def _(pe):
            pe.sem_inc(item_done, RING)

            def body(it, r, n, further=True):
                for k in range(RING):
                    pe.wait_ge(onehot_ready, n * RING + k + 1)
                    pe.wait_ge(added, n * RING + k + 1)
                    pe.wait_ge(gathered[k], n * 16 + 16)
                    nc.tensor.matmul(ps[:, k % 2, 0:W], onehot[:, k % 4, :], rows[:, k, 0:W], start=True, stop=True
                                     ).then_inc(item_done, 1)
            rounds(pe, body)


def mixing_stats(nc, a, b):
    wq, pw, wres = b.wq, b.pw, b.wres
    with ExitStack() as ctx:
        def sb(name, shape, dt=F32):
            return ctx.enter_context(nc.sbuf_tensor(name, shape, dt))

        sem = Sems(ctx, nc, "ms")
        xs = sb("ms_xs", [P, 2, 2, D])
        hx = sb("ms_hx", [P, 2, 2, D])
        hT = sb("ms_hT", [P, 2, 2, 2 * P])
        stats = sb("ms_stats", [P, 6, NPAIR, 6])
        mv = sb("ms_mv", [P, 6, 2])
        std = sb("ms_std", [P, 6])
        dw = sb("ms_dw", [P, 6])
        pT = ctx.enter_context(nc.psum_tensor("ms_pT", [P, 2, 2, 2 * P], F32))
        pq = ctx.enter_context(nc.psum_tensor("ms_pq", [P, 6, 2, 2 * P], F32))
        xs_in = [sem("xs_in0"), sem("xs_in1")]
        weights_in, pw_zero, std_ready, var_ready, chain = (sem("weights_in"), sem("pw_zero"), sem("std_ready"),
                                                            sem("var_ready"), sem("chain"))
        hx_step, tr_step, hT_step = Step(sem("hx"), 2), Step(sem("tr"), 2), Step(sem("hT"), 2)
        q_step, st_step = Step(sem("q"), 6, 3), Step(sem("st"), 6, 3)
        block = ctx.enter_context(nc.Block())

        @block.sync
        def _(sp):
            with nc.allow_non_contiguous_dma(reason="small weights"):
                sp.dma_start(wq[:, :, :], a["w_qkv"][2].rearrange("(k p) n -> p k n", p=P)).then_inc(weights_in, 16)
                sp.dma_start(dw[:, :], a["w_dw"][2].rearrange("o (m p) -> p (o m)", p=P)).then_inc(weights_in, 16)
                sp.dma_start(wres[:, :, :], a["w_res"].rearrange("(k p) n -> p k n", p=P)).then_inc(weights_in, 16)
                sp.wait_ge(pw_zero, 1)
                for g in range(4):
                    sp.dma_start(pw[32 * g:32 * g + 32, :, 32 * g:32 * g + 32],
                                 a["w_pw"].rearrange("(m g) i o -> g i m o", g=4)[g]).then_inc(weights_in, 16)

            def load(p, turn, place):
                hx_step.free(sp, p)
                sp.dma_start(xs[:, place], pairs(b.xn_d, p)).then_inc(xs_in[place], 16)
            over_pairs(sp, load)

        @block.scalar
        def _(act):
            hx_step.start(act)

            def scaled(p, turn, place):
                act.wait_ge(xs_in[place], turn * 16 + 16)
                tr_step.free(act, p)
                nc.scalar.activation(hx[:, place, 0], xs[:, place, 0], ACT.Identity, scale=b.scale_h[:, bass.ds(p * 2, 1)])
                hx_step.done(nc.scalar.activation(hx[:, place, 1], xs[:, place, 1], ACT.Identity,
                                                  scale=b.scale_h[:, bass.ds(p * 2 + 1, 1)]))
            over_pairs(act, scaled)
            act.wait_ge(var_ready, 1)
            nc.scalar.activation(std[:, :], std[:, :], ACT.Sqrt).then_inc(std_ready, 1)

        @block.tensor
        def _(pe):
            tr_step.start(pe)
            q_step.start(pe)
            pe.wait_ge(weights_in, 16 * 7)

            def front(p, turn, place):
                hx_step.after(pe, p)
                hT_step.free(pe, p)
                for k in range(2):
                    for j in range(2):
                        last = nc.tensor.transpose(pT[:, place, k, j * P:(j + 1) * P], hx[:, place, j, k * P:(k + 1) * P],
                                                   b.ident[:, :])
                tr_step.done(last)

            def main(p, turn, place):
                hT_step.after(pe, p)
                for c in range(3):
                    st_step.free(pe, p, c)
                    for m in (2 * c, 2 * c + 1):
                        for k in range(2):
                            last = nc.tensor.matmul(pq[:, 3 * place + c, m % 2, :], wq[:, k, m * P:(m + 1) * P],
                                                    hT[:, place, k, :], start=(k == 0), stop=(k == 1))
                    q_step.done(last)
            over_pairs_ahead(pe, front, main)

        @block.vector
        def _(dve):
            ch = Chain(dve, chain)
            hT_step.start(dve)
            st_step.start(dve)
            nc.vector.memset(pw[:, :, :], 0.0).then_inc(pw_zero, 1)
            dve.wait_ge(weights_in, 16 * 7)
            for m in range(6):
                nc.vector.tensor_scalar(pw[:, m, :], pw[:, m, :], dw[:, m:m + 1], None, ALU.mult)

            def front(p, turn, place):
                tr_step.after(dve, p)
                q_step_done_before(p)
                hT_step.done(nc.vector.tensor_copy(hT[:, place], pT[:, place]))

            def q_step_done_before(p):
                dve.wait_ge(q_step.sem, p * 3 + q_step.ring - 3)

            def main(p, turn, place, cols=2 * P):
                for c in range(3):
                    q_step.after(dve, p, c)
                    for m in (2 * c, 2 * c + 1):
                        last = nc.vector.bn_stats(flat(stats[:, m, bass.ds(p, 1), :]), pq[:, 3 * place + c, m % 2, 0:cols])
                    st_step.done(last)
            front(0, 0, 0)
            with dve.Fori(0, NPAIR // 2) as i:
                front(i * 2 + 1, i, 1)
                main(i * 2, i, 0)
                front(i * 2 + 2, i + 1, 0)
                main(i * 2 + 1, i, 1)
            main(NPAIR - 1, NPAIR // 2, 0, cols=N - (NPAIR - 1) * 2 * P)
            st_step.after(dve, NPAIR - 1, 2)
            for m in range(6):
                last = nc.vector.bn_aggr(mv[:, m, :], flat(stats[:, m]))
            ch.do(last)
            nc.vector.tensor_scalar(std[:, :], mv[:, :, 1], 1e-5, None, ALU.add).then_inc(var_ready, 1)
            dve.wait_ge(std_ready, 1)
            ch.do(nc.vector.reciprocal(std[:, :], std[:, :]))
            ch.do(nc.vector.tensor_tensor(b.bn_a[:, :], b.bn_a[:, :], std[:, :], ALU.mult))
            ch.do(nc.vector.tensor_tensor(std[:, :], mv[:, :, 0], b.bn_a[:, :], ALU.mult))
            ch.do(nc.vector.tensor_tensor(b.bn_b[:, :], b.bn_b[:, :], std[:, :], ALU.subtract))


def mixing(nc, a, b):
    wq, pw, wres, ident = b.wq, b.pw, b.wres, b.ident
    G = 16
    with ExitStack() as ctx:
        def sb(name, shape, dt=F32):
            return ctx.enter_context(nc.sbuf_tensor(name, shape, dt))

        sem = Sems(ctx, nc, "mx")
        xs = sb("mx_xs", [P, 2, 2, D])
        hx = sb("mx_hx", [P, 2, D])
        hT = sb("mx_hT", [P, 2, 2 * P])
        uT = sb("mx_uT", [P, 6, 2 * P])
        cat = sb("mx_cat", [P, 2, 2 * CH])
        squares = sb("mx_squares", [P, CH])
        nsq = sb("mx_nsq", [P, 2, 2])
        nrm = sb("mx_nrm", [P, 2, 2])
        sc = sb("mx_sc", [P, 8])
        al = sb("mx_al", [P, 2])
        ks = sb("mx_ks", [P, G])
        kr = sb("mx_kr", [P, G, 32])
        rv = sb("mx_rv", [P, G, 32])
        o = sb("mx_o", [P, 2, HID])
        osq = sb("mx_osq", [P, 2])
        onrm = sb("mx_onrm", [P, 2])
        oT = sb("mx_oT", [P, 4, P])
        ft = sb("mx_ft", [P, 2, 2, D])
        pT = ctx.enter_context(nc.psum_tensor("mx_pT", [P, 2, 2 * P], F32))
        pq = ctx.enter_context(nc.psum_tensor("mx_pq", [P, 2, 2, 2 * P], F32))
        pc = ctx.enter_context(nc.psum_tensor("mx_pc", [P, 2 * CH], F32))
        po = ctx.enter_context(nc.psum_tensor("mx_po", [P, 4, P], F32))
        pf = ctx.enter_context(nc.psum_tensor("mx_pf", [P, 512], F32))
        xs_in = [sem("xs_in0"), sem("xs_in1")]
        ft_out = [sem("ft_out0"), sem("ft_out1")]
        chain_v, chain_a = sem("chain_v"), sem("chain_a")
        hx_step = Step(sem("hx"), 1)
        tr_step = Step(sem("tr"), 1)
        hT_step = Step(sem("hT"), 1)
        q_step = Step(sem("q"), 2, 3)
        u_step = Step(sem("u"), 2, 3)
        c_step = Step(sem("c"), 1, 2)
        cs_step = Step(sem("cs"), 2, 2)
        o_step = Step(sem("o"), 2, 2)
        on_step = Step(sem("on"), 2, 2)
        ot_step = Step(sem("ot"), 2, 2)
        oT_step = Step(sem("oT"), 1, 2)
        f_step = Step(sem("f"), 1, 2)
        ft_step = Step(sem("ft"), 4, 2)
        fs_step = Step(sem("fs"), 4, 2)
        stored = Step(sem("stored"), 2)
        block = ctx.enter_context(nc.Block())

        @block.sync
        def _(sp):
            def load(p, turn, place, place_used=True):
                if place_used:
                    sp.wait_ge(hx_step.sem, p)
                sp.dma_start(xs[:, place], pairs(b.xn_d, p)).then_inc(xs_in[place], 16)

            def store(p, turn, place):
                ft_step.after(sp, p, 1)
                sp.dma_start(pairs(b.ft_d, p), ft[:, place]).then_inc(ft_out[place], 16)

            def landed(turn, place):
                sp.wait_ge(ft_out[place], turn * 16 + 16)
                sp.sem_inc(stored.sem, 1)
            stored.start(sp)
            load(0, 0, 0, place_used=False)
            load(1, 0, 1, place_used=False)
            with sp.Fori(0, NPAIR // 2 - 1) as i:
                for place in range(2):
                    store(i * 2 + place, i, place)
                    load(i * 2 + place + 2, i + 1, place)
                    landed(i, place)
            store(NPAIR - 3, NPAIR // 2 - 1, 0)
            load(NPAIR - 1, NPAIR // 2, 0)
            landed(NPAIR // 2 - 1, 0)
            store(NPAIR - 2, NPAIR // 2 - 1, 1)
            landed(NPAIR // 2 - 1, 1)
            store(NPAIR - 1, NPAIR // 2, 0)
            landed(NPAIR // 2, 0)

        @block.scalar
        def _(act):
            ch = Chain(act, chain_a)
            for s in (hx_step, hT_step, u_step, cs_step, on_step, oT_step, fs_step):
                s.start(act)

            def front(p, turn, place):
                ch.restart()
                act.wait_ge(xs_in[place], turn * 16 + 16)
                tr_step.free(act, p)
                nc.scalar.activation(hx[:, 0], xs[:, place, 0], ACT.Identity, scale=b.scale_h[:, bass.ds(p * 2, 1)])
                hx_step.done(nc.scalar.activation(hx[:, 1], xs[:, place, 1], ACT.Identity,
                                                  scale=b.scale_h[:, bass.ds(p * 2 + 1, 1)]))
                tr_step.after(act, p)
                act.wait_ge(q_step.sem, p * 3 + q_step.ring)
                hT_step.done(nc.scalar.copy(hT[:, :, :], pT[:, :, :]))
                act.wait_ge(c_step.sem, p * 2 + c_step.ring)
                for c in range(3):
                    q_step.after(act, p, c)
                    for m in (2 * c, 2 * c + 1):
                        last = nc.scalar.activation(uT[:, m, :], pq[:, (c + place) % 2, m % 2, :], ACT.Relu,
                                                    bias=b.bn_b[:, m:m + 1], scale=b.bn_a[:, m:m + 1])
                    u_step.done(last)
                fs_step.free(act, p, 1)
                for j in range(2):
                    c_step.after(act, p, j)
                    o_step.free(act, p, j)
                    ch.do(nc.scalar.activation(squares[:, :], pc[:, 0:CH], ACT.Square, accum_out=nsq[:, j, 0:1]))
                    ch.do(nc.scalar.activation(squares[:, :], pc[:, CH:2 * CH], ACT.Square, accum_out=nsq[:, j, 1:2]))
                    nc.scalar.activation(nrm[:, j, 0:1], nsq[:, j, 0:1], ACT.Sqrt)
                    nc.scalar.activation(nrm[:, j, 1:2], nsq[:, j, 1:2], ACT.Sqrt, bias=nsq[:, j, 0:1])
                    cs_step.done(nc.scalar.copy(cat[:, j, :], pc[:, :]))

            def main(p, turn, place):
                ch.restart()
                act.wait_ge(fs_step.sem, p * 2 + fs_step.ring)
                for j in range(2):
                    o_step.after(act, p, j)
                    ch.do(nc.scalar.activation(squares[:, 0:HID], o[:, j, :], ACT.Square, accum_out=osq[:, j:j + 1]))
                    act.wait_ge(ft_step.sem, p * 2 + (j + 3))
                    on_step.done(nc.scalar.activation(onrm[:, j:j + 1], osq[:, j:j + 1], ACT.Sqrt))
                    ot_step.after(act, p, j)
                    f_step.free(act, p, j)
                    oT_step.done(nc.scalar.copy(oT[:, :, :], po[:, :, :]))
                for j in range(2):
                    ft_step.after(act, p, j)
                    last = nc.scalar.activation(squares[:, 0:D], ft[:, place, j], ACT.Square,
                                                accum_out=b.ft_sq[:, bass.ds(p * 2 + j, 1)])
                    fs_step.done(last)
                    if j == 0:
                        fs_step.after(act, p, 0)
            over_pairs_ahead(act, front, main)

        @block.tensor
        def _(pe):
            for s in (tr_step, q_step, c_step, ot_step, f_step):
                s.start(pe)

            def front(p, turn, place):
                hx_step.after(pe, p)
                hT_step.free(pe, p)
                for k in range(2):
                    for j in range(2):
                        last = nc.tensor.transpose(pT[:, k, j * P:(j + 1) * P], hx[:, j, k * P:(k + 1) * P], ident[:, :])
                tr_step.done(last)
                hT_step.after(pe, p)
                for c in range(3):
                    u_step.free(pe, p, c)
                    for m in (2 * c, 2 * c + 1):
                        for k in range(2):
                            last = nc.tensor.matmul(pq[:, (c + place) % 2, m % 2, :], wq[:, k, m * P:(m + 1) * P],
                                                    hT[:, k, :], start=(k == 0), stop=(k == 1))
                    q_step.done(last)
                u_step.after(pe, p, 2)
                for j in range(2):
                    pe.wait_ge(cs_step.sem, p * 2 + j + cs_step.ring)
                    for m in range(6):
                        nc.tensor.transpose(pc[:, m * P:(m + 1) * P], uT[:, m, j * P:(j + 1) * P], ident[:, :])
                        last = nc.tensor.matmul(pc[:, CH + m * P:CH + (m + 1) * P], uT[:, m, j * P:(j + 1) * P],
                                                pw[:, m, :], start=True, stop=True)
                    c_step.done(last)

            def main(p, turn, place):
                for j in range(2):
                    o_step.after(pe, p, j)
                    oT_step.free(pe, p, j)
                    for k in range(4):
                        last = nc.tensor.transpose(po[:, k, :], o[:, j, k * P:(k + 1) * P], ident[:, :])
                    ot_step.done(last)
                    oT_step.after(pe, p, j)
                    pe.wait_ge(ft_step.sem, p * 2 + j + ft_step.ring)
                    for k in range(4):
                        last = nc.tensor.matmul(pf[:, 0:D], oT[:, k, :], wres[:, k, :], start=(k == 0), stop=(k == 3))
                    f_step.done(last)
            over_pairs_ahead(pe, front, main)

        @block.vector
        def _(dve):
            ch = Chain(dve, chain_v)
            o_step.start(dve)
            ft_step.start(dve)

            def factor(out_ap, n_ap, t):
                ch.do(nc.vector.tensor_scalar(t, n_ap, LOG_EPS, None, ALU.max))
                ch.do(nc.vector.reciprocal(t, t))
                ch.do(nc.vector.tensor_scalar(out_ap, n_ap, ATANH_MAX, t, ALU.min, ALU.mult))

            def front(p, turn, place):
                ch.restart()
                for j in range(2):
                    cs_step.after(dve, p, j)
                    factor(sc[:, 1:2], nrm[:, j, 0:1], sc[:, 0:1])
                    ch.do(nc.vector.tensor_tensor(sc[:, 2:3], sc[:, 1:2], nrm[:, j, 1:2], ALU.mult))
                    factor(sc[:, 4:5], sc[:, 2:3], sc[:, 3:4])
                    ch.do(nc.vector.tensor_tensor(al[:, 0:1], sc[:, 1:2], sc[:, 4:5], ALU.mult))
                    ch.do(nc.vector.tensor_tensor(al[:, 1:2], al[:, 0:1], al[:, 0:1], ALU.mult))
                    q, k, val = (cat[:, j, :].rearrange("p (g c e) -> p c g e", c=3, e=32)[:, c] for c in range(3))
                    ch.do(nc.vector.tensor_scalar(kr[:, :, :], k, 0.0, None, ALU.max))
                    nc.vector.tensor_reduce(out=ks[:, :], in_=kr[:, :, :], op=ALU.add, axis=AX.X)
                    ch.do(nc.vector.tensor_scalar(rv[:, :, :], val, al[:, 0:1], LOG_EPS, ALU.mult, ALU.add))
                    ch.do(nc.vector.reciprocal(rv[:, :, :], rv[:, :, :]))
                    nc.vector.scalar_tensor_tensor(out=rv[:, :, :], in0=val, scalar=al[:, 0:1], in1=rv[:, :, :],
                                                   op0=ALU.mult, op1=ALU.mult)
                    ch.do(nc.vector.scalar_tensor_tensor(out=kr[:, :, :], in0=q, scalar=0.0,
                                                         in1=ks[:, :].rearrange("p (g o) -> p g o", o=1).to_broadcast([P, G, 32]),
                                                         op0=ALU.max, op1=ALU.mult))
                    on_step.free(dve, p, j)
                    ot_step.free(dve, p, j)
                    o_step.done(nc.vector.scalar_tensor_tensor(
                        out=o[:, j, :].rearrange("p (g e) -> p g e", e=32), in0=kr[:, :, :], scalar=al[:, 1:2],
                        in1=rv[:, :, :], op0=ALU.mult, op1=ALU.mult))

            def main(p, turn, place):
                ch.restart()
                fs_step.free(dve, p, 1)
                stored.free(dve, p)
                for j in range(2):
                    on_step.after(dve, p, j)
                    factor(sc[:, 6:7], onrm[:, j:j + 1], sc[:, 5:6])
                    f_step.after(dve, p, j)
                    ft_step.done(nc.vector.scalar_tensor_tensor(out=ft[:, place, j], in0=pf[:, 0:D], scalar=sc[:, 6:7],
                                                                in1=b.bres_bc[:, :], op0=ALU.mult, op1=ALU.add))
            over_pairs_ahead(dve, front, main)


def sage_dense(nc, a, b):
    ident = b.ident
    with ExitStack() as ctx:
        def sb(name, shape, dt=F32):
            return ctx.enter_context(nc.sbuf_tensor(name, shape, dt))

        sem = Sems(ctx, nc, "sd")
        w1 = sb("sd_w1", [P, 4, HID])
        w2 = sb("sd_w2", [P, 4, 2 * D])
        xs = sb("sd_xs", [P, 2, 2, D])
        ag = sb("sd_ag", [P, 2, 2, D])
        inT = sb("sd_inT", [P, 4, 2 * P])
        hT = sb("sd_hT", [P, 4, 2 * P])
        ys = sb("sd_ys", [P, 2, 2, D])
        zs = sb("sd_zs", [P, 2, 2, D])
        pT = ctx.enter_context(nc.psum_tensor("sd_pT", [P, 4, 2 * P], F32))
        ph = ctx.enter_context(nc.psum_tensor("sd_ph", [P, 4, 2 * P], F32))
        py = ctx.enter_context(nc.psum_tensor("sd_py", [P, 2, 2, D], F32))
        weights_in, chain = sem("weights_in"), sem("chain")
        xs_in = [sem("xs_in0"), sem("xs_in1")]
        yz_out = [sem("yz_out0"), sem("yz_out1")]
        ag_step = Step(sem("ag"), 2)
        tr_step = Step(sem("tr"), 2)
        in_step = Step(sem("in"), 1)
        h_step = Step(sem("h"), 2, 2)
        hT_step = Step(sem("hT"), 2, 2)
        y_step = Step(sem("y"), 2, 2)
        out_step = Step(sem("out"), 4, 2)
        stored = Step(sem("stored"), 2)
        block = ctx.enter_context(nc.Block())

        @block.sync
        def _(sp):
            for dst, src in ((w1[:, 0:2, :], a["W1l"]), (w1[:, 2:4, :], a["W1r"]),
                             (w2[:, :, 0:D], a["W2l"]), (w2[:, :, D:2 * D], a["W2r"])):
                sp.dma_start(dst, src.rearrange("(k p) n -> p k n", p=P)).then_inc(weights_in, 16)

            def load(p, turn, place, place_used=True):
                if place_used:
                    tr_step.free(sp, p)
                sp.dma_start(xs[:, place], pairs(b.xn_d, p)).then_inc(xs_in[place], 16)

            def store(p, turn, place):
                out_step.after(sp, p, 1)
                sp.dma_start(pairs(b.y_d, p), ys[:, place]).then_inc(yz_out[place], 16)
                sp.dma_start(pairs(b.z_d, p), zs[:, place]).then_inc(yz_out[place], 16)

            def landed(turn, place):
                sp.wait_ge(yz_out[place], turn * 32 + 32)
                sp.sem_inc(stored.sem, 1)
            stored.start(sp)
            load(0, 0, 0, place_used=False)
            load(1, 0, 1, place_used=False)
            with sp.Fori(0, NPAIR // 2 - 1) as i:
                for place in range(2):
                    load(i * 2 + place + 2, i + 1, place)
                    store(i * 2 + place, i, place)
                    landed(i, place)
            load(NPAIR - 1, NPAIR // 2, 0)
            store(NPAIR - 3, NPAIR // 2 - 1, 0)
            landed(NPAIR // 2 - 1, 0)
            store(NPAIR - 2, NPAIR // 2 - 1, 1)
            landed(NPAIR // 2 - 1, 1)
            store(NPAIR - 1, NPAIR // 2, 0)
            landed(NPAIR // 2, 0)

        @block.vector
        def _(dve):
            ch = Chain(dve, chain)
            ag_step.start(dve)
            out_step.start(dve)
            ch.do(nc.vector.tensor_scalar(b.rdeg[:, :], b.acc[:, :, D], 1.0, None, ALU.max))
            ch.do(nc.vector.reciprocal(b.rdeg[:, :], b.rdeg[:, :]))

            def front(p, turn, place):
                tr_step.free(dve, p)
                for j in range(2):
                    last = nc.vector.tensor_scalar(ag[:, place, j], flat(b.acc[:, bass.ds(p * 2 + j, 1), 0:D]),
                                                   b.rdeg[:, bass.ds(p * 2 + j, 1)], None, ALU.mult)
                ag_step.done(last)

            def main(p, turn, place):
                stored.free(dve, p)
                for j in range(2):
                    y_step.after(dve, p, j)
                    nc.vector.tensor_copy(ys[:, place, j], py[:, j, 0])
                    out_step.done(nc.vector.tensor_tensor(zs[:, place, j], py[:, j, 1], b.b2_bc[:, :], ALU.add))
            over_pairs_ahead(dve, front, main)

        @block.scalar
        def _(act):
            in_step.start(act)
            hT_step.start(act)

            def body(p, turn, place):
                tr_step.after(act, p)
                act.wait_ge(h_step.sem, p * 2 + h_step.ring)
                in_step.done(nc.scalar.copy(inT[:, :, :], pT[:, :, :]))
                act.wait_ge(y_step.sem, p * 2 + y_step.ring)
                for c in range(2):
                    h_step.after(act, p, c)
                    for m in (2 * c, 2 * c + 1):
                        last = nc.scalar.activation(hT[:, m, :], ph[:, m, :], ACT.Relu, bias=b.b1[:, m:m + 1])
                    hT_step.done(last)
            over_pairs(act, body)

        @block.tensor
        def _(pe):
            tr_step.start(pe)
            h_step.start(pe)
            y_step.start(pe)
            pe.wait_ge(weights_in, 64)

            def front(p, turn, place):
                pe.wait_ge(xs_in[place], turn * 16 + 16)
                ag_step.after(pe, p)
                in_step.free(pe, p)
                for k in range(4):
                    src = (ag, ag, xs, xs)[k]
                    for j in range(2):
                        last = nc.tensor.transpose(pT[:, k, j * P:(j + 1) * P],
                                                   src[:, place, j, k % 2 * P:(k % 2 + 1) * P], ident[:, :])
                tr_step.done(last)

            def main(p, turn, place):
                in_step.after(pe, p)
                for c in range(2):
                    hT_step.free(pe, p, c)
                    for m in (2 * c, 2 * c + 1):
                        for k in range(4):
                            last = nc.tensor.matmul(ph[:, m, :], w1[:, k, m * P:(m + 1) * P], inT[:, k, :],
                                                    start=(k == 0), stop=(k == 3))
                    h_step.done(last)
                hT_step.after(pe, p, 1)
                for j in range(2):
                    pe.wait_ge(out_step.sem, p * 2 + j - 1 + out_step.ring)
                    for k in range(4):
                        last = nc.tensor.matmul(flat(py[:, j]), hT[:, k, j * P:(j + 1) * P], w2[:, k, :],
                                                start=(k == 0), stop=(k == 3))
                    y_step.done(last)
            over_pairs_ahead(pe, front, main)


def finish(nc, a, b, out):
    ident, X = b.ident, b.X
    outer = ExitStack()
    with outer:
        def keep(name, shape, dt=F32):
            return outer.enter_context(nc.sbuf_tensor(name, shape, dt))

        moe_w1 = keep("moe_w1", [P, NE, 2, D])
        moe_w2 = keep("moe_w2", [P, NE, 2, D])
        TT = keep("TT", [P, 2, NROWS])
        weight = keep("weight", [P, NT2, NE])
        moe_in = outer.enter_context(nc.semaphore("moe_in"))

        with ExitStack() as ctx:
            def sb(name, shape, dt=F32):
                return ctx.enter_context(nc.sbuf_tensor(name, shape, dt))

            sem = Sems(ctx, nc, "to")
            xr = sb("to_xr", [P, 2, 2, D])
            zr = sb("to_zr", [P, 2, 2, D])
            fr = sb("to_fr", [P, 2, 2, D])
            x1 = sb("to_x1", [P, 2, D])
            ts = sb("to_ts", [P, 2, D])
            tT = sb("to_tT", [P, 2, 2 * P])
            stats = sb("to_stats", [P, 2, 6])
            mv = sb("to_mv", [P, 2, 2])
            std = sb("to_std", [P, 2])
            f_n = sb("to_f_n", [P, NT2])
            f_t = sb("to_f_t", [P, NT2])
            pT = ctx.enter_context(nc.psum_tensor("to_pT", [P, 2, 2 * P], F32))
            pl = ctx.enter_context(nc.psum_tensor("to_pl", [P, 2, NE], F32))
            rows_in = [sem("rows_in0"), sem("rows_in1")]
            chain, fn_ready, ft_ready, softmax_in, exp_ready = (sem("chain"), sem("fn_ready"), sem("ft_ready"),
                                                                sem("softmax_in"), sem("exp_ready"))
            used_step = Step(sem("used"), 2)
            var_step = Step(sem("var"), 1)
            std_step = Step(sem("std"), 1)
            ts_step = Step(sem("ts"), 1)
            tr_step = Step(sem("tr"), 1)
            tT_step = Step(sem("tT"), 1)
            l_step = Step(sem("l"), 1)
            lo_step = Step(sem("lo"), 1)
            block = ctx.enter_context(nc.Block())

            @block.sync
            def _(sp):
                def load(p, turn, place, place_used=True):
                    if place_used:
                        used_step.free(sp, p)
                    for dst, src in ((xr, b.xp_d), (zr, b.z_d), (fr, b.ft_d)):
                        sp.dma_start(dst[:, place], pairs(src, p)).then_inc(rows_in[place], 16)
                load(0, 0, 0, place_used=False)
                load(1, 0, 1, place_used=False)
                for e in range(NE):
                    sp.dma_start(moe_w1[:, e], a["ew1"][e].rearrange("(k p) n -> p k n", p=P)).then_inc(moe_in, 16)
                    sp.dma_start(moe_w2[:, e], a["ew2"][e].rearrange("(k p) n -> p k n", p=P)).then_inc(moe_in, 16)
                with sp.Fori(1, NPAIR // 2) as i:
                    load(i * 2, i, 0)
                    load(i * 2 + 1, i, 1)
                load(NPAIR - 1, NPAIR // 2, 0)

            @block.scalar
            def _(act):
                nc.scalar.activation(f_n[:, :], b.ft_sq[:, :], ACT.Sqrt).then_inc(fn_ready, 1)
                act.wait_ge(fn_ready, 1)
                nc.scalar.activation(f_t[:, :], f_n[:, :], ACT.Tanh).then_inc(ft_ready, 1)
                std_step.start(act)
                tT_step.start(act)

                def body(p, turn, place):
                    var_step.after(act, p)
                    std_step.done(nc.scalar.activation(std[:, :], std[:, :], ACT.Sqrt))
                    tr_step.after(act, p)
                    l_step.free(act, p)
                    lo_step.free(act, p)
                    tT_step.done(nc.scalar.copy(tT[:, :, :], pT[:, :, :]))
                over_pairs(act, body)
                act.wait_ge(softmax_in, 1)
                nc.scalar.activation(weight[:, :, :], weight[:, :, :], ACT.Exp).then_inc(exp_ready, 1)

            @block.tensor
            def _(pe):
                tr_step.start(pe)
                l_step.start(pe)

                def body(p, turn, place):
                    ts_step.after(pe, p)
                    tT_step.free(pe, p)
                    for k in range(2):
                        for j in range(2):
                            last = nc.tensor.transpose(pT[:, k, j * P:(j + 1) * P], ts[:, j, k * P:(k + 1) * P], ident[:, :])
                    tr_step.done(last)
                    tT_step.after(pe, p)
                    lo_step.free(pe, p)
                    for j in range(2):
                        for k in range(2):
                            last = nc.tensor.matmul(pl[:, j, :], tT[:, k, j * P:(j + 1) * P], b.router[:, k, :],
                                                    start=(k == 0), stop=(k == 1))
                    l_step.done(last)
                over_pairs(pe, body)

            @block.vector
            def _(dve):
                ch = Chain(dve, chain)
                for s in (used_step, var_step, ts_step, lo_step):
                    s.start(dve)
                dve.wait_ge(ft_ready, 1)
                ch.do(nc.vector.tensor_scalar(f_n[:, :], f_n[:, :], LOG_EPS, None, ALU.max))
                ch.do(nc.vector.reciprocal(f_n[:, :], f_n[:, :]))
                ch.do(nc.vector.scalar_tensor_tensor(out=f_t[:, :], in0=f_t[:, :], scalar=MAXNORM, in1=f_n[:, :],
                                                     op0=ALU.min, op1=ALU.mult))

                def body(p, turn, place):
                    ch.restart()
                    lo_step.free(dve, p)
                    dve.wait_ge(rows_in[place], turn * 48 + 48)
                    ch.do(nc.vector.tensor_tensor(x1[:, :, :], xr[:, place], zr[:, place], ALU.add))
                    for j in range(2):
                        last = nc.vector.scalar_tensor_tensor(
                            out=x1[:, j], in0=fr[:, place, j], scalar=f_t[:, bass.ds(p * 2 + j, 1)], in1=x1[:, j],
                            op0=ALU.mult, op1=ALU.add)
                    used_step.done(last)
                    used_step.after(dve, p)
                    for j in range(2):
                        last = nc.vector.scalar_tensor_tensor(
                            out=x1[:, j], in0=flat(b.acc[:, bass.ds(p * 2 + j, 1), 0:D]),
                            scalar=b.rdeg[:, bass.ds(p * 2 + j, 1)], in1=x1[:, j], op0=ALU.mult, op1=ALU.add)
                    ch.do(last)
                    for j in range(2):
                        last = nc.vector.bn_stats(stats[:, j, :], x1[:, j])
                    ch.do(last)
                    for j in range(2):
                        last = nc.vector.bn_aggr(mv[:, j, :], stats[:, j, :])
                    ch.do(last)
                    var_step.done(nc.vector.tensor_scalar(std[:, :], mv[:, :, 1], LN_EPS, None, ALU.add))
                    std_step.after(dve, p)
                    ch.do(nc.vector.reciprocal(std[:, :], std[:, :]))
                    tr_step.free(dve, p)
                    for j in range(2):
                        last = nc.vector.tensor_scalar(ts[:, j], x1[:, j], mv[:, j, 0:1], std[:, j:j + 1],
                                                       ALU.subtract, ALU.mult)
                    ts_step.done(last)
                    ts_step.after(dve, p)
                    nc.vector.tensor_tensor(X[:, bass.ds(p * 2, 2), :], x1[:, :, :], ts[:, :, :], ALU.add)
                    tT_step.after(dve, p)
                    nc.vector.tensor_copy(TT[:, :, bass.ds(p * 2 * P, 2 * P)], tT[:, :, :])
                    l_step.after(dve, p)
                    lo_step.done(nc.vector.tensor_copy(weight[:, bass.ds(p * 2, 2), :], pl[:, :, :]))
                over_pairs(dve, body)
                lo_step.after(dve, NPAIR - 1)
                ch.restart()
                w = weight[:, :, :]
                big = fr[:, :, :, :].rearrange("p a b c -> p (a b c)")
                tmp = [big[:, i * NT2 * NE:(i + 1) * NT2 * NE].rearrange("p (t e) -> p t e", e=NE) for i in range(2)]
                big2 = zr[:, :, :, :].rearrange("p a b c -> p (a b c)")
                rank, picked = (big2[:, i * NT2 * NE:(i + 1) * NT2 * NE].rearrange("p (t e) -> p t e", e=NE)
                                for i in range(2))
                red = f_n[:, :]

                def wide(ap):
                    return ap.rearrange("p (t o) -> p t o", o=1).to_broadcast([P, NT2, NE])

                for e in range(NE):
                    last = nc.vector.memset(rank[:, :, e], float(NE - e))
                ch.do(last)
                ch.do(nc.vector.tensor_reduce(out=red, in_=w, op=ALU.max, axis=AX.X))
                nc.vector.tensor_tensor(w, w, wide(red), ALU.subtract).then_inc(softmax_in, 1)
                dve.wait_ge(exp_ready, 1)
                ch.do(nc.vector.tensor_reduce(out=red, in_=w, op=ALU.add, axis=AX.X))
                ch.do(nc.vector.reciprocal(red, red))
                ch.do(nc.vector.tensor_tensor(w, w, wide(red), ALU.mult))
                ch.do(nc.vector.tensor_copy(tmp[0], w))
                for turn in range(2):
                    ch.do(nc.vector.tensor_reduce(out=red, in_=tmp[0], op=ALU.max, axis=AX.X))
                    ch.do(nc.vector.tensor_tensor(tmp[1], tmp[0], wide(red), ALU.is_equal))
                    ch.do(nc.vector.tensor_tensor(tmp[1], tmp[1], rank, ALU.mult))
                    ch.do(nc.vector.tensor_reduce(out=red, in_=tmp[1], op=ALU.max, axis=AX.X))
                    ch.do(nc.vector.tensor_tensor(tmp[1], rank, wide(red), ALU.is_equal))
                    if turn == 0:
                        ch.do(nc.vector.tensor_copy(picked, tmp[1]))
                        ch.do(nc.vector.scalar_tensor_tensor(out=tmp[0], in0=tmp[1], scalar=-2.0, in1=tmp[0],
                                                             op0=ALU.mult, op1=ALU.add))
                    else:
                        ch.do(nc.vector.tensor_tensor(picked, picked, tmp[1], ALU.add))
                ch.do(nc.vector.tensor_tensor(w, w, picked, ALU.mult))
                ch.do(nc.vector.tensor_reduce(out=red, in_=w, op=ALU.add, axis=AX.X))
                ch.do(nc.vector.tensor_scalar(red, red, 1e-12, None, ALU.max))
                ch.do(nc.vector.reciprocal(red, red))
                ch.do(nc.vector.tensor_tensor(w, w, wide(red), ALU.mult))

        with ExitStack() as ctx:
            def sb(name, shape, dt=F32):
                return ctx.enter_context(nc.sbuf_tensor(name, shape, dt))

            sem = Sems(ctx, nc, "ex")
            gT = sb("ex_gT", [P, 2, 2, 2 * P])
            cs = sb("ex_cs", [P, 2, 2, NE])
            cT = sb("ex_cT", [NE, 2 * P])
            ph = ctx.enter_context(nc.psum_tensor("ex_ph", [P, 2, 2, 2 * P], F32))
            py = ctx.enter_context(nc.psum_tensor("ex_py", [P, 2, 2, D], F32))
            pc = ctx.enter_context(nc.psum_tensor("ex_pc", [P, 512], F32))
            pb = ctx.enter_context(nc.psum_tensor("ex_pb", [P, 2, D], F32))
            out_done, chain = sem("out_done"), sem("chain")
            h_step = Step(sem("h"), 2, NE)
            g_step = Step(sem("g"), 2, NE)
            y_step = Step(sem("y"), 2, NE)
            add_step = Step(sem("add"), 2, NE)
            cs_step = Step(sem("cs"), 2)
            ct_step = Step(sem("ct"), 1)
            cT_step = Step(sem("cT"), 1)
            bias_step = Step(sem("bias"), 1)
            fin_step = Step(sem("fin"), 1)
            block = ctx.enter_context(nc.Block())

            @block.sync
            def _(sp):
                def store(p, turn, place):
                    fin_step.after(sp, p)
                    sp.dma_start(pairs(out, p), X[:, bass.ds(p * 2, 2), :]).then_inc(out_done, 16)
                with sp.Fori(0, NPAIR - 1) as p:
                    store(p, 0, 0)
                fin_step.after(sp, NPAIR - 1)
                sp.dma_start(out[(NT - 1) * P:N, :], X[0:LAST, NT - 1, :]).then_inc(out_done, 16)
                sp.wait_ge(out_done, 16 * NPAIR)

            @block.tensor
            def _(pe):
                for s in (h_step, y_step, ct_step, bias_step):
                    s.start(pe)
                pe.wait_ge(moe_in, 16 * 2 * NE)

                def first(p, e):
                    g_step.free(pe, p, e)
                    for m in range(2):
                        for k in range(2):
                            last = nc.tensor.matmul(ph[:, e % 2, m], moe_w1[:, e, k, m * P:(m + 1) * P],
                                                    TT[:, k, bass.ds(p * 2 * P, 2 * P)], start=(k == 0), stop=(k == 1))
                    h_step.done(last)

                def second(p, e):
                    g_step.after(pe, p, e)
                    add_step.free(pe, p, e)
                    for j in range(2):
                        for k in range(2):
                            last = nc.tensor.matmul(py[:, e % 2, j], gT[:, e % 2, k, j * P:(j + 1) * P], moe_w2[:, e, k, :],
                                                    start=(k == 0), stop=(k == 1))
                    y_step.done(last)

                def body(p, turn, place, last_pair=False):
                    cs_step.after(pe, p)
                    cT_step.free(pe, p)
                    for j in range(2):
                        last = nc.tensor.transpose(pc[0:NE, j * P:(j + 1) * P], cs[:, place, j, :], ident[:, :])
                    ct_step.done(last)
                    for e in range(NE):
                        if e + 1 < NE:
                            first(p, e + 1)
                        elif not last_pair:
                            first(p + 1, 0)
                        second(p, e)
                    cT_step.after(pe, p)
                    fin_step.free(pe, p)
                    for j in range(2):
                        last = nc.tensor.matmul(pb[:, j], cT[0:NE, j * P:(j + 1) * P], b.moe_b2[:, :], start=True, stop=True)
                    bias_step.done(last)

                first(0, 0)
                with pe.Fori(0, NPAIR // 2) as i:
                    body(i * 2, i, 0)
                    body(i * 2 + 1, i, 1)
                body(NPAIR - 1, NPAIR // 2, 0, last_pair=True)

            @block.scalar
            def _(act):
                g_step.start(act)
                cT_step.start(act)

                def body(p, turn, place):
                    for e in range(NE):
                        h_step.after(act, p, e)
                        y_step.free(act, p, e)
                        for m in range(2):
                            last = nc.scalar.activation(gT[:, e % 2, m, :], ph[:, e % 2, m], ACT.Gelu,
                                                        bias=b.moe_b1[:, e, m:m + 1])
                        g_step.done(last)
                        if e == 3:
                            ct_step.after(act, p)
                            bias_step.free(act, p)
                            cT_step.done(nc.scalar.copy(cT[:, :], pc[0:NE, 0:2 * P]))
                over_pairs(act, body)

            @block.vector
            def _(dve):
                add_step.start(dve)
                cs_step.start(dve)
                fin_step.start(dve)

                def stage(p, turn, place):
                    dve.wait_ge(ct_step.sem, p)
                    cs_step.done(nc.vector.tensor_copy(cs[:, place], weight[:, bass.ds(p * 2, 2), :]))

                def body(p, turn, place, last_pair=False):
                    for e in range(NE):
                        y_step.after(dve, p, e)
                        dve.wait_ge(add_step.sem, p * NE + e + add_step.ring)
                        for j in range(2):
                            at = flat(X[:, bass.ds(p * 2 + j, 1), :])
                            last = nc.vector.scalar_tensor_tensor(
                                out=at, in0=py[:, e % 2, j], scalar=flat(weight[:, bass.ds(p * 2 + j, 1), e:e + 1]),
                                in1=at, op0=ALU.mult, op1=ALU.add)
                        add_step.done(last)
                    if not last_pair:
                        stage(p + 1, turn + place, 1 - place)
                    bias_step.after(dve, p)
                    add_step.after(dve, p, NE - 1)
                    at = X[:, bass.ds(p * 2, 2), :]
                    fin_step.done(nc.vector.tensor_tensor(at, at, pb[:, :, :], ALU.add))
                cs_step.done(nc.vector.tensor_copy(cs[:, 0], weight[:, 0:2, :]))
                with dve.Fori(0, NPAIR // 2) as i:
                    body(i * 2, i, 0)
                    body(i * 2 + 1, i, 1)
                body(NPAIR - 1, NPAIR // 2, 0, last_pair=True)


def kernel(**inputs):
    import numpy as np
    import concourse.bacc as bacc
    from concourse.bass_utils import run_bass_kernel_spmd

    laid_out = {
        "x": inputs["x"], "src": inputs["src"], "dst": inputs["dst"],
        "W1l": inputs["L0_gnn_W1l"], "b1": inputs["L0_gnn_b1"], "W1r": inputs["L0_gnn_W1r"],
        "W2l": inputs["L0_gnn_W2l"], "b2": inputs["L0_gnn_b2"], "W2r": inputs["L0_gnn_W2r"],
        "w_qkv": np.transpose(inputs["L0_mix_w_qkv"], (2, 1, 0)),
        "gamma": inputs["L0_mix_bn_gamma"], "beta": inputs["L0_mix_bn_beta"],
        "w_dw": np.transpose(inputs["L0_mix_w_dw"], (2, 1, 0)),
        "w_pw": np.transpose(np.reshape(inputs["L0_mix_w_pw"], (CH // 32, 32, 32)), (0, 2, 1)),
        "w_res": np.transpose(np.reshape(inputs["L0_mix_w_res"], (D, HID)), (1, 0)),
        "b_res": inputs["L0_mix_b_res"], "routerT": np.transpose(inputs["L0_ffn_router_w"], (1, 0)),
        "ew1": inputs["L0_ffn_w1"], "eb1": inputs["L0_ffn_b1"], "ew2": inputs["L0_ffn_w2"], "eb2": inputs["L0_ffn_b2"],
    }
    nc = bacc.Bacc("TRN2", target_bir_lowering=False, num_devices=1)
    arrays, a = {}, {}
    for name, value in laid_out.items():
        value = np.ascontiguousarray(value)
        arrays[f"in_{name}"] = value
        a[name] = nc.dram_tensor(f"in_{name}", value.shape, mybir.dt.from_np(value.dtype), kind="ExternalInput").ap()
    out = nc.dram_tensor("out_0", (N, D), F32, kind="ExternalOutput").ap()
    gnn_mix_moe(nc, a, out)
    r = run_bass_kernel_spmd(nc, [arrays], core_ids=[0])
    return r.results[0]["out_0"]
```

```python
from contextlib import ExitStack

import concourse.bass as bass
from concourse import mybir

F32 = mybir.dt.float32
I32 = mybir.dt.int32
ALU = mybir.AluOpType
ACT = mybir.ActivationFunctionType
AX = mybir.AxisListType
P = 128

N = 6250
E = 200000
D = 256
HID = 512
CH = 768
NT = -(-N // P)
NPAIR = (NT + 1) // 2
NT2 = 2 * NPAIR
NROWS = NT2 * P
LAST = N - (NT - 1) * P
ET = -(-E // P)
RING = 16
BANK = RING // 2
ITER = -(-(ET + NT - 1) // RING)
ITEMS = ITER * RING
assert ITER > 4 * NPAIR
AHEAD = 2
IC = -(-ITEMS // P)
IPAD = IC * P
NE = 8
ACCW = D + 1

MAXNORM = 1.0 - 1e-5
ATANH_MAX = 6.1023555
LOG_EPS = 1e-15
LN_EPS = 1e-5


class Buffers:
    pass


class Sems:

    def __init__(self, ctx, nc, prefix):
        self.ctx, self.nc, self.prefix = ctx, nc, prefix

    def __call__(self, name):
        return self.ctx.enter_context(self.nc.semaphore(f"{self.prefix}_{name}"))


class Chain:

    def __init__(self, eng, sem):
        self.eng, self.sem, self.n = eng, sem, 0

    def restart(self):
        self.eng.sem_clear(self.sem)
        self.n = 0

    def do(self, ins):
        self.n += 1
        ins.then_inc(self.sem, 1)
        self.eng.wait_ge(self.sem, self.n)


class Step:

    def __init__(self, sem, ring, per=1):
        self.sem, self.ring, self.per = sem, ring, per

    def start(self, eng):
        eng.sem_inc(self.sem, self.ring)

    def done(self, ins):
        ins.then_inc(self.sem, 1)

    def after(self, eng, p, c=0):
        eng.wait_ge(self.sem, p * self.per + (c + 1 + self.ring))

    def free(self, eng, p, c=0):
        eng.wait_ge(self.sem, p * self.per + (c + 1))


def pairs(ap, p):
    return ap[bass.ds(p * 2 * P, 2 * P), :].rearrange("(j q) f -> q j f", q=P)


def flat(ap):
    return ap.rearrange("p a w -> p (a w)")


def over_pairs(eng, body):
    with eng.Fori(0, NPAIR // 2) as i:
        body(i * 2, i, 0)
        body(i * 2 + 1, i, 1)
    body(NPAIR - 1, NPAIR // 2, 0)


def over_pairs_ahead(eng, front, main):
    front(0, 0, 0)
    with eng.Fori(0, NPAIR // 2) as i:
        front(i * 2 + 1, i, 1)
        main(i * 2, i, 0)
        front(i * 2 + 2, i + 1, 0)
        main(i * 2 + 1, i, 1)
    main(NPAIR - 1, NPAIR // 2, 0)


def gnn_mix_moe(nc, a, out):
    top = ExitStack()
    b = Buffers()
    with top:
        def sbuf(ctx, name, shape, dt=F32):
            return ctx.enter_context(nc.sbuf_tensor(name, shape, dt))

        def psum(ctx, name, shape):
            return ctx.enter_context(nc.psum_tensor(name, shape, F32))

        def scratch(name, shape, dt=F32):
            return nc.dram_tensor(name, shape, dt, kind="Internal").ap()

        b.xp_d = scratch("xp_d", (NROWS, D))
        b.xn_d = scratch("xn_d", (NROWS + 2 * P, D))
        b.y_d = scratch("y_d", (NROWS, D))
        b.z_d = scratch("z_d", (NROWS, D))
        b.ft_d = scratch("ft_d", (NROWS, D))
        b.srcp_d = scratch("srcp_d", (IPAD, P), I32)
        b.dstp_d = scratch("dstp_d", (IPAD, P), I32)
        b.blk_d = scratch("blk_d", (IC, P), I32)

        early = ExitStack()
        b.acc = sbuf(top, "acc", [P, NT2, ACCW])
        b.ident = sbuf(top, "ident", [P, P])
        b.scale_h = sbuf(top, "scale_h", [P, NT2])
        b.ft_sq = sbuf(top, "ft_sq", [P, NT2])
        b.rdeg = sbuf(top, "rdeg", [P, NT2])
        b.b2_bc = sbuf(top, "b2_bc", [P, D])
        b.bres_bc = sbuf(top, "bres_bc", [P, D])
        b.b1 = sbuf(top, "b1", [P, 4])
        b.moe_b1 = sbuf(top, "moe_b1", [P, NE, 2])
        b.moe_b2 = sbuf(top, "moe_b2", [NE, D])
        b.router = sbuf(top, "router", [P, 2, NE])
        b.bn_a = sbuf(top, "bn_a", [P, 6])
        b.bn_b = sbuf(top, "bn_b", [P, 6])
        b.sorted_f = sbuf(top, "sorted_f", [P, 1])
        b.unsorted_i = sbuf(top, "unsorted_i", [1, 1], I32)
        b.srcT = sbuf(early, "srcT", [P, IPAD], I32)
        b.dstT = sbuf(early, "dstT", [P, IPAD])
        b.blk_row = sbuf(early, "blk_row", [1, IPAD], I32)
        b.ready_row = sbuf(early, "ready_row", [1, ITER], I32)
        b.iota = sbuf(early, "iota", [P, P])
        b.rows = sbuf(early, "rows", [P, RING, ACCW])
        b.onehot = sbuf(early, "onehot", [P, 4, P])
        b.ix = sbuf(early, "ix", [P, RING], I32)

        with ExitStack() as first:
            b.X = sbuf(first, "X", [P, NT2, D])
            setup(nc, a, b)
        first_layer(nc, a, b)
        aggregate(nc, "g2", b.y_d, b, with_degree=False)
        early.close()
        b.X = sbuf(top, "X2", [P, NT2, D])
        finish(nc, a, b, out)


def setup(nc, a, b):
    X, xn_d, ident, iota = b.X, b.xn_d, b.ident, b.iota
    srcp_d, dstp_d, blk_d = b.srcp_d, b.dstp_d, b.blk_d
    srcT, dstT, blk_row, rows, scale_h = b.srcT, b.dstT, b.blk_row, b.rows, b.scale_h
    sorted_f, unsorted_i = b.sorted_f, b.unsorted_i
    PADE = IPAD * P - E
    PR = 116
    assert PADE % PR == 0
    CHK = 100
    CL = E // CHK
    with ExitStack() as ctx:
        used = [0]

        def sb(name, shape, dt=F32):
            words = shape[1] * (shape[2] if len(shape) == 3 else 1)
            t = acc[0:shape[0], used[0]:used[0] + words]
            used[0] += words
            if dt is not F32:
                t = t.bitcast(dt)
            return t.rearrange("p (a w) -> p a w", w=shape[2]) if len(shape) == 3 else t

        acc = b.acc[:, :, :].rearrange("p t w -> p (t w)")
        sem = Sems(ctx, nc, "su")
        fill0 = sb("fill0", [PR, PADE // PR], I32)
        fillm = sb("fillm", [PR, PADE // PR], I32)
        zrow = sb("zrow", [50, (NROWS - N) // 50 * D])
        chk = sb("chk", [CHK, CL + 1], I32)
        viol = sb("viol", [CHK, 1])
        ones = sb("ones", [P, P])
        last_i = sb("last_i", [1, ET], I32)
        key = last_i.bitcast(F32)
        tix = sb("tix", [1, ET])
        item_f = sb("item_f", [P, IC])
        tile_f = sb("tile_f", [P, IC])
        tile_i = sb("tile_i", [P, IC], I32)
        blk_f = sb("blk_f", [P, IC])
        blk_i = sb("blk_i", [P, IC], I32)
        junk = sb("junk", [P, CL])
        itS = sb("itS", [P, IC, P], I32)
        itD = sb("itD", [P, IC, P], I32)
        stats = sb("stats", [P, NT2, 6])
        mv = sb("mv", [P, NT2, 2])
        rstd = sb("rstd", [P, NT2])
        nrm = sb("nrm", [P, NT2])
        t1 = sb("t1", [P, NT2])
        t2 = sb("t2", [P, NT2])
        t3 = sb("t3", [P, NT2])
        sq_out = sb("sq_out", [P, D])
        itSf = itS[:, :, :].bitcast(F32)
        itDf = itD[:, :, :].bitcast(F32)

        key_ps = ctx.enter_context(nc.psum_tensor("key_ps", [P, 2048], F32))
        tr_ps = ctx.enter_context(nc.psum_tensor("tr_ps", [P, 2, 512], F32))
        sum_ps = ctx.enter_context(nc.psum_tensor("sum_ps", [P, 8], F32))

        xp_out = sem("xp_out")
        fills, padded, x_in, last_in, chk_in = sem("fills"), sem("padded"), sem("x_in"), sem("last_in"), sem("chk_in")
        weights_in, consts, chk_set = sem("weights_in"), sem("consts"), sem("chk_set")
        viol_ready, viol_sum, key_ready, key_bc = sem("viol_ready"), sem("viol_sum"), sem("key_ready"), sem("key_bc")
        tiles_ready, blk_ready, blk_out, items_in = sem("tiles_ready"), sem("blk_ready"), sem("blk_out"), sem("items_in")
        tabs_ready, tr_done, tr_used, blk_back = sem("tabs_ready"), sem("tr_done"), sem("tr_used"), sem("blk_back")
        var_ready, std_ready, xn_ready, sq_ready, nrm_ready = (sem("var_ready"), sem("std_ready"), sem("xn_ready"),
                                                              sem("sq_ready"), sem("nrm_ready"))
        lnin_ready, ln_ready, xn_out, zeroed = sem("lnin_ready"), sem("ln_ready"), sem("xn_out"), sem("zeroed")
        chain_v, chain_p, chain_a = sem("chain_v"), sem("chain_p"), sem("chain_a")
        block = ctx.enter_context(nc.Block())

        @block.sync
        def _(sp):
            with nc.allow_non_contiguous_dma(reason="last edge of each tile; small tables"):
                sp.wait_ge(zeroed, 1)
                sp.dma_start(X[:, 0:NT - 1, :], a["x"][0:(NT - 1) * P, :].rearrange("(t p) f -> p t f", p=P)
                             ).then_inc(x_in, 16)
                sp.dma_start(X[0:LAST, NT - 1, :], a["x"][(NT - 1) * P:N, :]).then_inc(x_in, 16)
                sp.dma_start(b.xp_d[0:N, :].rearrange("(q r) f -> q (r f)", q=50), a["x"].rearrange("(q r) f -> q (r f)", q=50)
                             ).then_inc(xp_out, 16)
                sp.wait_ge(fills, 3)
                sp.dma_start(b.xp_d[N:NROWS, :].rearrange("(q r) f -> q (r f)", q=50), zrow[:, :]).then_inc(xp_out, 16)
                sp.dma_start(last_i[0:1, 0:ET - 1], a["dst"][0:(ET - 1) * P].rearrange("(o t p) -> o t p", o=1, p=P)[:, :, P - 1]
                             ).then_inc(last_in, 16)
                sp.dma_start(last_i[0:1, ET - 1:ET], a["dst"][E - 1:E].rearrange("(o t) -> o t", o=1)).then_inc(last_in, 16)
                sp.wait_ge(chk_set, 1)
                sp.dma_start(chk[:, 0:CL], a["dst"].rearrange("(p c) -> p c", p=CHK)).then_inc(chk_in, 16)
                sp.dma_start(chk[0:CHK - 1, CL:CL + 1], a["dst"][CL:E].rearrange("(p c) -> p c", c=CL)[:, 0:1]
                             ).then_inc(chk_in, 16)
                for d, s, f in ((srcp_d, a["src"], fill0), (dstp_d, a["dst"], fillm)):
                    flat = d.rearrange("t p -> (t p)")
                    sp.dma_start(flat[0:E].rearrange("(q n) -> q n", q=16), s.rearrange("(q n) -> q n", q=16)
                                 ).then_inc(padded, 16)
                    sp.wait_ge(fills, 2)
                    sp.dma_start(flat[E:IPAD * P].rearrange("(q n) -> q n", q=PR), f[:, :]).then_inc(padded, 16)
                loads = [
                    (b.b1[:, :], a["b1"].rearrange("(k p) -> p k", p=P)),
                    (b.b2_bc[:, :], a["b2"].rearrange("(o n) -> o n", o=1).to_broadcast([P, D])),
                    (b.bres_bc[:, :], a["b_res"].rearrange("(o n) -> o n", o=1).to_broadcast([P, D])),
                    (b.router[:, :, :], a["routerT"].rearrange("(k p) e -> p k e", p=P)),
                    (b.moe_b1[:, :, :], a["eb1"].rearrange("e (m p) -> p e m", p=P)),
                    (b.moe_b2[:, :], a["eb2"]),
                    (b.bn_a[:, :], a["gamma"].rearrange("(m p) -> p m", p=P)),
                    (b.bn_b[:, :], a["beta"].rearrange("(m p) -> p m", p=P)),
                ]
                for dst, src in loads:
                    sp.dma_start(dst, src).then_inc(weights_in, 16)
                sp.wait_ge(blk_ready, 1)
                sp.dma_start(blk_d.rearrange("c p -> p c"), blk_i[:, :]).then_inc(blk_out, 16)
                sp.wait_ge(blk_out, 16)
                sp.dma_start(blk_row[0:1, :], blk_d.rearrange("c p -> (c p)").rearrange("(o n) -> o n", o=1)
                             ).then_inc(blk_back, 16)
                sp.wait_ge(xn_ready, 1)
                sp.dma_start(xn_d[0:NROWS, :].rearrange("(t p) f -> p t f", p=P), X[:, :, :]).then_inc(xn_out, 16)
                sp.dma_start(xn_d[NROWS:NROWS + 2 * P, :].rearrange("(t p) f -> p t f", p=P), X[:, 0:2, :]).then_inc(xn_out, 16)
                sp.wait_ge(xn_out, 32)
                sp.wait_ge(xp_out, 32)
                sp.wait_ge(blk_back, 16)
                sp.wait_ge(weights_in, 16 * len(loads))

        @block.gpsimd
        def _(pool):
            ch = Chain(pool, chain_p)
            pool.memset(fill0[:, :], 0).then_inc(fills, 1)
            pool.memset(fillm[:, :], -1).then_inc(fills, 1)
            pool.memset(zrow[:, :], 0.0).then_inc(fills, 1)
            pool.memset(chk[:, :], 1 << 23).then_inc(chk_set, 1)
            ch.do(pool.memset(ident[:, :], 0.0))
            ch.do(pool.affine_select(out=ident[:, :], in_=ident[:, :], compare_op=ALU.not_equal, fill=1.0, base=0,
                                     pattern=[[-1, P]], channel_multiplier=1))
            pool.iota(iota[:, :], pattern=[[1, P]], base=0, channel_multiplier=0, allow_small_or_imprecise_dtypes=True
                      ).then_inc(consts, 1)
            pool.iota(tix[:, :], pattern=[[1, ET]], base=0, channel_multiplier=0, allow_small_or_imprecise_dtypes=True
                      ).then_inc(consts, 1)
            pool.iota(item_f[:, :], pattern=[[P, IC]], base=0, channel_multiplier=1, allow_small_or_imprecise_dtypes=True
                      ).then_inc(consts, 1)
            pool.memset(ones[:, :], 1.0).then_inc(consts, 1)
            pool.memset(rows[:, :, D:D + 1], 1.0).then_inc(consts, 1)
            pool.wait_ge(tiles_ready, 1)
            pool.wait_ge(padded, 64)
            for table, d in ((itS, srcp_d), (itD, dstp_d)):
                for c in range(IC):
                    pool.indirect_dma_start(table[:, c, :], None, d[:, :],
                                            bass.IndirectOffsetOnAxis(ap=tile_i[:, c:c + 1], axis=0)
                                            ).then_inc(items_in, 16)

        @block.vector
        def _(dve):
            ch = Chain(dve, chain_v)
            nc.vector.memset(X[:, NT - 1:NT2, :], 0.0).then_inc(zeroed, 1)
            dve.wait_ge(chk_in, 32)
            ch.do(nc.vector.tensor_tensor(junk[0:CHK, :], chk[:, 0:CL], chk[:, 1:CL + 1], ALU.is_gt))
            nc.vector.tensor_reduce(out=viol[:, :], in_=junk[0:CHK, :], op=ALU.add, axis=AX.X).then_inc(viol_ready, 1)
            dve.wait_ge(viol_sum, 1)
            nc.vector.tensor_scalar(unsorted_i[0:1, 0:1], sum_ps[0:1, 0:1], 0.5, None, ALU.is_gt)
            ch.do(nc.vector.tensor_scalar(sorted_f[:, :], sum_ps[:, 0:1], 0.5, None, ALU.is_lt))
            dve.wait_ge(last_in, 32)
            dve.wait_ge(consts, 5)
            ch.do(nc.vector.tensor_scalar(last_i[:, :], last_i[:, :], 0.0, float(NT * P - 1), ALU.max, ALU.min))
            ch.do(nc.vector.tensor_scalar(last_i[:, :], last_i[:, :], 7, None, ALU.arith_shift_right))
            nc.vector.scalar_tensor_tensor(out=key[:, :], in0=last_i[:, :], scalar=sorted_f[0:1, 0:1], in1=tix[:, :],
                                           op0=ALU.mult, op1=ALU.add).then_inc(key_ready, 1)
            dve.wait_ge(key_bc, 1)
            for c in range(IC):
                ch.do(nc.vector.tensor_scalar(junk[:, 0:ET], key_ps[:, 0:ET], item_f[:, c:c + 1], None, ALU.is_lt,
                                              ALU.add, accum_out=tile_f[:, c:c + 1]))
            nc.vector.tensor_copy(tile_i[:, :], tile_f[:, :]).then_inc(tiles_ready, 1)
            ch.do(nc.vector.tensor_tensor(blk_f[:, :], item_f[:, :], tile_f[:, :], ALU.subtract))
            ch.do(nc.vector.tensor_scalar(blk_f[:, :], blk_f[:, :], float(NT - 1), sorted_f[:, 0:1], ALU.min, ALU.mult))
            ch.do(nc.vector.tensor_copy(blk_i[:, :], blk_f[:, :]))
            dve.sem_inc(blk_ready, 1)
            ch.do(nc.vector.tensor_scalar(blk_f[:, :], blk_f[:, :], float(P), None, ALU.mult))
            dve.wait_ge(x_in, 32)
            for t in range(NT2):
                last = nc.vector.bn_stats(stats[:, t, :], X[:, t, :])
            ch.do(last)
            for t in range(NT2):
                last = nc.vector.bn_aggr(mv[:, t, :], stats[:, t, :])
            ch.do(last)
            nc.vector.tensor_scalar(rstd[:, :], mv[:, :, 1], LN_EPS, None, ALU.add).then_inc(var_ready, 1)
            dve.wait_ge(std_ready, 1)
            ch.do(nc.vector.reciprocal(rstd[:, :], rstd[:, :]))
            for t in range(NT2):
                last = nc.vector.tensor_scalar(X[:, t, :], X[:, t, :], mv[:, t, 0:1], rstd[:, t:t + 1],
                                               ALU.subtract, ALU.mult)
            last.then_inc(xn_ready, 1)
            dve.wait_ge(items_in, 16 * 2 * IC)
            for c in range(IC):
                nc.vector.tensor_scalar(itDf[:, c, :], itD[:, c, :], blk_f[:, c:c + 1], None, ALU.subtract)
                last = nc.vector.tensor_copy(itSf[:, c, :], itS[:, c, :])
            last.then_inc(tabs_ready, 1)
            for c in range(IC):
                dve.wait_ge(tr_done, c + 1)
                nc.vector.tensor_copy(srcT[:, c * P:(c + 1) * P], tr_ps[:, c % 2, 0:P])
                nc.vector.tensor_copy(dstT[:, c * P:(c + 1) * P], tr_ps[:, c % 2, P:2 * P]).then_inc(tr_used, 1)
            dve.wait_ge(tr_used, IC)
            nc.vector.tensor_copy(srcT[:, ITEMS:ITEMS + BANK], srcT[:, 0:BANK])
            nc.vector.tensor_scalar(dstT[:, ITEMS:ITEMS + AHEAD], dstT[:, 0:AHEAD], float(P), None, ALU.subtract)
            dve.wait_ge(blk_back, 16)
            nc.vector.tensor_scalar(b.ready_row[0:1, :], blk_row[0:1, 0:ITEMS:RING], 1, None, ALU.arith_shift_right)
            dve.wait_ge(nrm_ready, 1)
            ch.do(nc.vector.tensor_scalar(t1[:, :], nrm[:, :], MAXNORM, None, ALU.min))
            ch.do(nc.vector.tensor_scalar(t2[:, :], t1[:, :], 1.0, None, ALU.add))
            ch.do(nc.vector.tensor_scalar(t3[:, :], t1[:, :], -1.0, 1.0, ALU.mult, ALU.add))
            ch.do(nc.vector.reciprocal(t3[:, :], t3[:, :]))
            nc.vector.tensor_tensor(t2[:, :], t2[:, :], t3[:, :], ALU.mult).then_inc(lnin_ready, 1)
            dve.wait_ge(ln_ready, 1)
            ch.do(nc.vector.tensor_scalar(nrm[:, :], nrm[:, :], LOG_EPS, None, ALU.max))
            ch.do(nc.vector.reciprocal(t3[:, :], nrm[:, :]))
            ch.do(nc.vector.scalar_tensor_tensor(out=scale_h[:, :], in0=t2[:, :], scalar=0.5, in1=t3[:, :],
                                                 op0=ALU.mult, op1=ALU.mult))
            ch.do(nc.vector.tensor_scalar(nrm[:, :], t1[:, :], 0.1, None, ALU.is_lt))
            ch.do(nc.vector.tensor_tensor(t2[:, :], t1[:, :], t1[:, :], ALU.mult))
            ch.do(nc.vector.tensor_tensor(t3[:, :], t1[:, :], t3[:, :], ALU.mult))
            ch.do(nc.vector.tensor_scalar(t1[:, :], t2[:, :], 1.0 / 7, 1.0 / 5, ALU.mult, ALU.add))
            ch.do(nc.vector.tensor_tensor(t1[:, :], t1[:, :], t2[:, :], ALU.mult))
            ch.do(nc.vector.tensor_scalar(t1[:, :], t1[:, :], 1.0 / 3, None, ALU.add))
            ch.do(nc.vector.tensor_tensor(t1[:, :], t1[:, :], t2[:, :], ALU.mult))
            ch.do(nc.vector.tensor_scalar(t1[:, :], t1[:, :], 1.0, None, ALU.add))
            ch.do(nc.vector.tensor_tensor(t1[:, :], t1[:, :], t3[:, :], ALU.mult))
            ch.do(nc.vector.tensor_tensor(t1[:, :], t1[:, :], scale_h[:, :], ALU.subtract))
            ch.do(nc.vector.tensor_tensor(t1[:, :], t1[:, :], nrm[:, :], ALU.mult))
            ch.do(nc.vector.tensor_tensor(scale_h[:, :], scale_h[:, :], t1[:, :], ALU.add))

        @block.scalar
        def _(act):
            act.wait_ge(var_ready, 1)
            nc.scalar.activation(rstd[:, :], rstd[:, :], ACT.Sqrt).then_inc(std_ready, 1)
            act.wait_ge(xn_ready, 1)
            ch = Chain(act, chain_a)
            for t in range(NT2):
                ch.do(nc.scalar.activation(sq_out[:, :], X[:, t, :], ACT.Square, accum_out=nrm[:, t:t + 1]))
            nc.scalar.activation(nrm[:, :], nrm[:, :], ACT.Sqrt).then_inc(nrm_ready, 1)
            act.wait_ge(lnin_ready, 1)
            nc.scalar.activation(t2[:, :], t2[:, :], ACT.Ln).then_inc(ln_ready, 1)

        @block.tensor
        def _(pe):
            pe.wait_ge(consts, 5)
            pe.wait_ge(viol_ready, 1)
            nc.tensor.matmul(sum_ps[:, 0:1], ones[0:CHK, :], viol[:, :], start=True, stop=True).then_inc(viol_sum, 1)
            pe.wait_ge(key_ready, 1)
            for c in range(0, ET, 512):
                n = min(512, ET - c)
                last = nc.tensor.matmul(key_ps[:, c:c + n], ones[0:1, :], key[0:1, c:c + n], start=True, stop=True)
            last.then_inc(key_bc, 1)
            pe.wait_ge(tabs_ready, 1)
            for c in range(IC):
                if c >= 2:
                    pe.wait_ge(tr_used, c - 1)
                nc.tensor.transpose(tr_ps[:, c % 2, 0:P], itSf[:, c, :], ident[:, :])
                nc.tensor.transpose(tr_ps[:, c % 2, P:2 * P], itDf[:, c, :], ident[:, :]).then_inc(tr_done, 1)


class Items:

    def __init__(self, nc, ctx, name, table_d, b, with_degree):
        sem = Sems(ctx, nc, name)
        self.nc, self.b, self.table_d = nc, b, table_d
        self.W = ACCW if with_degree else D
        self.ps = ctx.enter_context(nc.psum_tensor(f"{name}_ps", [P, 2, 512], F32))
        self.gathered = [sem(f"gathered{k}") for k in range(RING)]
        self.bank_ready = [sem(f"bank_ready{k}") for k in range(2)]
        self.onehot_ready, self.item_done, self.added = sem("onehot_ready"), sem("item_done"), sem("added")
        self.zeroed, self.shifted = sem("zeroed"), sem("shifted")
        self.blks = None

    def pool_half(self, pool, it, n, bank):
        rows, ix = self.b.rows, self.b.ix
        pool.wait_ge(self.bank_ready[bank], 1)
        pool.sem_clear(self.bank_ready[bank])
        for k in range(bank * BANK, (bank + 1) * BANK):
            pool.indirect_dma_start(rows[:, k, 0:D], None, self.table_d[:, :],
                                    bass.IndirectOffsetOnAxis(ap=ix[:, k:k + 1], axis=0)).then_inc(self.gathered[k], 16)

    def act_start(self, act):
        self.nc.scalar.copy(self.b.ix[:, 0:BANK], self.b.srcT[:, 0:BANK]).then_inc(self.bank_ready[0], 1)

    def act_half(self, act, it, n, bank):
        act.wait_ge(self.item_done, n * RING + (bank * BANK + RING))
        other = 1 - bank
        self.nc.scalar.copy(self.b.ix[:, other * BANK:(other + 1) * BANK],
                            self.b.srcT[:, bass.ds(it * RING + (bank + 1) * BANK, BANK)]).then_inc(self.bank_ready[other], 1)

    def onehot(self, dve, it, n, k):
        dve.wait_ge(self.item_done, n * RING + (k + 1 + RING - 4))
        self.nc.vector.tensor_scalar(self.b.onehot[:, k % 4, :], self.b.iota[:, :], self.b.dstT[:, bass.ds(it * RING + k, 1)],
                                     None, ALU.is_equal).then_inc(self.onehot_ready, 1)

    def dve_start(self, dve):
        self.nc.vector.memset(self.b.acc[:, :, 0:self.W], 0.0).then_inc(self.zeroed, 1)
        dve.wait_ge(self.zeroed, 1)
        dve.sem_inc(self.added, 2)
        for k in range(AHEAD):
            self.onehot(dve, 0, 0, k)

    def dve_half(self, dve, it, n, bank, r=None):
        if bank == 0:
            self.blks = [r] * RING if r is not None else self.nc.values_load_multi_w_load_instructions(
                self.b.blk_row[0:1, bass.ds(it * RING, RING)], engines=(mybir.EngineType.DVE,), min_val=0,
                max_val=NT - 1, skip_runtime_bounds_check_because="setup clamps the table")[1]
        for k in range(bank * BANK, (bank + 1) * BANK):
            self.onehot(dve, it, n, k + AHEAD)
            at = flat(self.b.acc[:, bass.ds(self.blks[k], 1), 0:self.W])
            dve.wait_ge(self.item_done, n * RING + (k + 1 + RING))
            dve.wait_ge(self.added, n * RING + (k + 2))
            self.nc.vector.tensor_tensor(at, at, self.ps[:, k % 2, 0:self.W], ALU.add).then_inc(self.added, 1)
        if bank == 1:
            dve.wait_ge(self.added, n * RING + (RING + 2))

    def pe_start(self, pe):
        pe.sem_inc(self.item_done, RING)

    def pe_half(self, pe, it, n, bank):
        for k in range(bank * BANK, (bank + 1) * BANK):
            pe.wait_ge(self.onehot_ready, n * RING + (k + 1))
            pe.wait_ge(self.added, n * RING + (k + 1))
            pe.wait_ge(self.gathered[k], n * 16 + 16)
            self.nc.tensor.matmul(self.ps[:, k % 2, 0:self.W], self.b.onehot[:, k % 4, :], self.b.rows[:, k, 0:self.W],
                                  start=True, stop=True).then_inc(self.item_done, 1)

    def further_rounds(self, eng, half, between=None, after=None):
        flag = eng.value_load(self.b.unsorted_i[0:1, 0:1], min_val=0, max_val=1)
        with eng.If(flag > 0):
            with eng.Fori(1, NT) as r:
                if between:
                    between()
                with eng.Fori(0, ITER) as it:
                    for bank in range(2):
                        half(it, r * ITER + it, bank, r)
            if after:
                after()

    def pool_rounds(self, pool):
        with pool.Fori(0, ITER) as it:
            for bank in range(2):
                self.pool_half(pool, it, it, bank)
        self.further_rounds(pool, lambda it, n, bank, r: self.pool_half(pool, it, n, bank))

    def act_rounds(self, act):
        self.further_rounds(act, lambda it, n, bank, r: self.act_half(act, it, n, bank))

    def pe_rounds(self, pe):
        self.further_rounds(pe, lambda it, n, bank, r: self.pe_half(pe, it, n, bank))

    def dve_rounds(self, dve):
        ch = Chain(dve, self.shifted)

        def shift(by):
            ch.restart()
            ch.do(self.nc.vector.tensor_scalar(self.b.dstT[:, :], self.b.dstT[:, :], by, None, ALU.add))
        self.further_rounds(dve, lambda it, n, bank, r: self.dve_half(dve, it, n, bank, r),
                            between=lambda: shift(-float(P)), after=lambda: shift(float(P * (NT - 1))))


def ready_pairs(eng, b, before, after, job):
    if after is None:
        lo = eng.value_load(b.ready_row[0:1, before:before + 1], min_val=0, max_val=NPAIR - 1)
        with eng.Fori(lo, NPAIR) as p:
            job(p)
        return
    lo = eng.value_load(b.ready_row[0:1, bass.ds(before, 1)], min_val=0, max_val=NPAIR - 1)
    hi = eng.value_load(b.ready_row[0:1, bass.ds(after, 1)], min_val=0, max_val=NPAIR - 1)
    with eng.If(hi > lo):
        with eng.Fori(lo, hi) as p:
            job(p)


def first_layer(nc, a, b):
    ident = b.ident
    G = 16
    with ExitStack() as ctx:
        def sb(name, shape, dt=F32):
            return ctx.enter_context(nc.sbuf_tensor(name, shape, dt))

        sem = Sems(ctx, nc, "fl")
        items = Items(nc, ctx, "g1", b.xn_d, b, with_degree=True)
        wq = sb("wq", [P, 2, CH])
        pw = sb("pw", [P, 6, P])
        wres = sb("wres", [P, 4, D])
        dw = sb("dw", [P, 6])
        xs = sb("xs", [P, 2, 2, D])
        hx = sb("hx", [P, 2, D])
        hT = sb("hT", [P, 2, 2 * P])
        stats = sb("stats", [P, 6, NPAIR, 6])
        mv = sb("mv", [P, 6, 2])
        std = sb("std", [P, 6])
        uT = sb("uT", [P, 6, 2 * P])
        cat = sb("cat", [P, 2, 2 * CH])
        squares = sb("squares", [P, CH])
        nsq = sb("nsq", [P, 2, 2])
        nrm = sb("nrm", [P, 2, 2])
        sc = sb("sc", [P, 8])
        al = sb("al", [P, 2])
        ks = sb("ks", [P, G])
        kr = sb("kr", [P, G, 32])
        rv = sb("rv", [P, G, 32])
        o = sb("o", [P, 2, HID])
        osq = sb("osq", [P, 2])
        onrm = sb("onrm", [P, 2])
        oT = sb("oT", [P, 4, P])
        ft = sb("ft", [P, 2, D])
        w1 = sb("w1", [P, 4, HID])
        w2 = sb("w2", [P, 4, 2 * D])
        xg = sb("xg", [P, 2, D])
        ag = sb("ag", [P, 2, D])
        inT = sb("inT", [P, 4, 2 * P])
        gT = sb("gT", [P, 4, 2 * P])
        ys = sb("ys", [P, 2, D])
        zs = sb("zs", [P, 2, D])
        R = ctx.enter_context(nc.psum_tensor("fl_R", [P, 6, 2, 2 * P], F32))
        Rw = R[:, :, :, :].rearrange("p r a w -> p (r a w)")
        pT, po = R[:, 0], R[:, 0].rearrange("p a (c w) -> p (a c) w", w=P)
        pc = Rw[:, 3 * 512:6 * 512]
        pf = Rw[:, 512:512 + D]
        dT = Rw[:, 0:2 * 512].rearrange("p (k w) -> p k w", k=4)
        dh = Rw[:, 2 * 512:4 * 512].rearrange("p (k w) -> p k w", k=4)
        dy = R[:, 4:6]

        xs_in = [sem("xs_in0"), sem("xs_in1")]
        weights_in, pw_zero, var_ready, std_ready, bn_ready = (sem("weights_in"), sem("pw_zero"), sem("var_ready"),
                                                               sem("std_ready"), sem("bn_ready"))
        ft_out, xg_in, yz_out, yz_open = sem("ft_out"), sem("xg_in"), sem("yz_out"), sem("yz_open")
        chain_v, chain_a = sem("chain_v"), sem("chain_a")
        hx_step = Step(sem("hx"), 1)
        tr_step = Step(sem("tr"), 1)
        hT_step = Step(sem("hT"), 1)
        sq_step = Step(sem("sq"), 3, 3)
        st_step = Step(sem("st"), 3, 3)
        q_step = Step(sem("q"), 2, 3)
        u_step = Step(sem("u"), 2, 3)
        c_step = Step(sem("c"), 1, 2)
        cs_step = Step(sem("cs"), 2, 2)
        o_step = Step(sem("o"), 2, 2)
        on_step = Step(sem("on"), 2, 2)
        ot_step = Step(sem("ot"), 2, 2)
        oT_step = Step(sem("oT"), 1, 2)
        f_step = Step(sem("f"), 1, 2)
        ft_step = Step(sem("ft"), 2, 2)
        fs_step = Step(sem("fs"), 2, 2)
        stored = Step(sem("stored"), 1)
        ag_step = Step(sem("ag"), 1)
        dt_step = Step(sem("dt"), 1)
        in_step = Step(sem("in"), 1)
        h_step = Step(sem("h"), 2, 2)
        gT_step = Step(sem("gT"), 2, 2)
        y_step = Step(sem("y"), 2, 2)
        out_step = Step(sem("out"), 2, 2)
        block = ctx.enter_context(nc.Block())
        MIX = NPAIR
        S_TURNS, M_TURNS = NPAIR, 3 * NPAIR

        def schedule(eng, half, stats_half, bn, mix_half, dense_job):
            def stats_turn(p, turn, place):
                for bank in range(2):
                    half(p, p, bank)
                    stats_half(p, turn, place, bank)
                ready_pairs(eng, b, p, p + 1, dense_job)

            def mix_turns(p, turn, place):
                for s in range(3):
                    for bank in range(2):
                        t = p * 3 + (S_TURNS + s)
                        half(t, t, bank)
                        mix_half(p, turn, place, 2 * s + bank)
                ready_pairs(eng, b, p * 3 + S_TURNS, p * 3 + (S_TURNS + 3), dense_job)

            over_pairs(eng, stats_turn)
            bn()
            over_pairs(eng, mix_turns)
            with eng.Fori(S_TURNS + M_TURNS, ITER) as t:
                for bank in range(2):
                    half(t, t, bank)

        @block.sync
        def _(sp):
            with nc.allow_non_contiguous_dma(reason="small weights"):
                sp.dma_start(wq[:, :, :], a["w_qkv"][2].rearrange("(k p) n -> p k n", p=P)).then_inc(weights_in, 16)
                sp.dma_start(dw[:, :], a["w_dw"][2].rearrange("o (m p) -> p (o m)", p=P)).then_inc(weights_in, 16)
                sp.dma_start(wres[:, :, :], a["w_res"].rearrange("(k p) n -> p k n", p=P)).then_inc(weights_in, 16)
                for dst, src in ((w1[:, 0:2, :], a["W1l"]), (w1[:, 2:4, :], a["W1r"]),
                                 (w2[:, :, 0:D], a["W2l"]), (w2[:, :, D:2 * D], a["W2r"])):
                    sp.dma_start(dst, src.rearrange("(k p) n -> p k n", p=P)).then_inc(weights_in, 16)
                sp.wait_ge(pw_zero, 1)
                for g in range(4):
                    sp.dma_start(pw[32 * g:32 * g + 32, :, 32 * g:32 * g + 32],
                                 a["w_pw"].rearrange("(m g) i o -> g i m o", g=4)[g]).then_inc(weights_in, 16)

            def load(p, place, q, place_used=True):
                if place_used:
                    sp.wait_ge(hx_step.sem, q)
                sp.dma_start(xs[:, place], pairs(b.xn_d, p)).then_inc(xs_in[place], 16)

            def store(p):
                ft_step.after(sp, p, 1)
                sp.dma_start(pairs(b.ft_d, p), ft[:, :, :]).then_inc(ft_out, 16)
                sp.wait_ge(ft_out, p * 16 + 16)
                sp.sem_inc(stored.sem, 1)
            stored.start(sp)
            load(0, 0, 0, place_used=False)
            load(1, 1, 1, place_used=False)
            with sp.Fori(1, NPAIR // 2) as i:
                load(i * 2, 0, i * 2)
                load(i * 2 + 1, 1, i * 2 + 1)
            load(NPAIR - 1, 0, NPAIR - 1)
            load(0, 1, MIX)
            load(1, 0, MIX + 1)
            with sp.Fori(0, NPAIR // 2 - 1) as i:
                for k in range(2):
                    load(i * 2 + 2 + k, 1 - k, i * 2 + (2 + k + MIX))
                    store(i * 2 + k)
            load(NPAIR - 1, 1, NPAIR - 1 + MIX)
            for k in range(3):
                store(NPAIR - 3 + k)

        @block.gpsimd
        def _(pool):
            items.pool_rounds(pool)

        @block.tensor
        def _(pe):
            items.pe_start(pe)
            for s in (tr_step, sq_step, q_step, c_step, ot_step, f_step, dt_step, h_step, y_step):
                s.start(pe)
            pe.wait_ge(weights_in, 16 * 11)

            def transpose_rows(q):
                hx_step.after(pe, q)
                hT_step.free(pe, q)
                for k in range(2):
                    for j in range(2):
                        last = nc.tensor.transpose(pT[:, k, j * P:(j + 1) * P], hx[:, j, k * P:(k + 1) * P], ident[:, :])
                tr_step.done(last)

            def stats_half(p, turn, place, bank):
                if bank == 0:
                    transpose_rows(p)
                    return
                hT_step.after(pe, p)
                for c in range(3):
                    st_step.free(pe, p, c)
                    for m in (2 * c, 2 * c + 1):
                        for k in range(2):
                            last = nc.tensor.matmul(R[:, 1 + c, m % 2, :], wq[:, k, m * P:(m + 1) * P], hT[:, k, :],
                                                    start=(k == 0), stop=(k == 1))
                    sq_step.done(last)

            def mix_half(p, turn, place, h):
                if h == 0:
                    pe.wait_ge(oT_step.sem, p * 2 + oT_step.ring)
                    transpose_rows(p + MIX)
                if h == 1:
                    hT_step.after(pe, p + MIX)
                    pe.wait_ge(ft_step.sem, p * 2 + ft_step.ring)
                    for c in range(3):
                        u_step.free(pe, p, c)
                        for m in (2 * c, 2 * c + 1):
                            for k in range(2):
                                last = nc.tensor.matmul(R[:, 1 + (c + place) % 2, m % 2, :], wq[:, k, m * P:(m + 1) * P],
                                                        hT[:, k, :], start=(k == 0), stop=(k == 1))
                        q_step.done(last)
                if h in (2, 3):
                    j = h - 2
                    u_step.after(pe, p, 2)
                    pe.wait_ge(cs_step.sem, p * 2 + (j + cs_step.ring))
                    for m in range(6):
                        nc.tensor.transpose(pc[:, m * P:(m + 1) * P], uT[:, m, j * P:(j + 1) * P], ident[:, :])
                        last = nc.tensor.matmul(pc[:, CH + m * P:CH + (m + 1) * P], uT[:, m, j * P:(j + 1) * P],
                                                pw[:, m, :], start=True, stop=True)
                    c_step.done(last)
                if h in (4, 5):
                    j = h - 4
                    o_step.after(pe, p, j)
                    oT_step.free(pe, p, j)
                    for k in range(4):
                        last = nc.tensor.transpose(po[:, k, :], o[:, j, k * P:(k + 1) * P], ident[:, :])
                    ot_step.done(last)
                    oT_step.after(pe, p, j)
                    pe.wait_ge(ft_step.sem, p * 2 + (j + ft_step.ring))
                    for k in range(4):
                        last = nc.tensor.matmul(pf, oT[:, k, :], wres[:, k, :], start=(k == 0), stop=(k == 3))
                    f_step.done(last)

            def dense_job(p):
                pe.wait_ge(xg_in, p * 16 + 16)
                ag_step.after(pe, p)
                for k in range(4):
                    src = (ag, ag, xg, xg)[k]
                    for j in range(2):
                        last = nc.tensor.transpose(dT[:, k, j * P:(j + 1) * P], src[:, j, k % 2 * P:(k % 2 + 1) * P],
                                                   ident[:, :])
                dt_step.done(last)
                in_step.after(pe, p)
                for c in range(2):
                    for m in (2 * c, 2 * c + 1):
                        for k in range(4):
                            last = nc.tensor.matmul(dh[:, m, :], w1[:, k, m * P:(m + 1) * P], inT[:, k, :],
                                                    start=(k == 0), stop=(k == 3))
                    h_step.done(last)
                gT_step.after(pe, p, 1)
                for j in range(2):
                    for k in range(4):
                        last = nc.tensor.matmul(flat(dy[:, j]), gT[:, k, j * P:(j + 1) * P], w2[:, k, :],
                                                start=(k == 0), stop=(k == 3))
                    y_step.done(last)
                out_step.after(pe, p, 1)

            schedule(pe, lambda it, n, bank: items.pe_half(pe, it, n, bank), stats_half,
                     lambda: st_step.after(pe, NPAIR - 1, 2), mix_half, dense_job)
            items.pe_rounds(pe)
            ready_pairs(pe, b, S_TURNS + M_TURNS, None, dense_job)

        @block.scalar
        def _(act):
            ch = Chain(act, chain_a)
            items.act_start(act)
            for s in (hx_step, hT_step, u_step, cs_step, on_step, oT_step, fs_step, in_step, gT_step):
                s.start(act)
            act.wait_ge(yz_open, 1)
            act.dma_start(pairs(b.y_d, 0), ys[:, :, :]).then_inc(yz_out, 16)
            act.dma_start(pairs(b.z_d, 0), zs[:, :, :]).then_inc(yz_out, 16)
            act.dma_start(xg[:, :, :], pairs(b.xn_d, 0)).then_inc(xg_in, 16)

            def scale_rows(p, q, place, arrived):
                act.wait_ge(xs_in[place], arrived)
                tr_step.free(act, q)
                nc.scalar.activation(hx[:, 0], xs[:, place, 0], ACT.Identity, scale=b.scale_h[:, bass.ds(p * 2, 1)])
                hx_step.done(nc.scalar.activation(hx[:, 1], xs[:, place, 1], ACT.Identity,
                                                  scale=b.scale_h[:, bass.ds(p * 2 + 1, 1)]))
                tr_step.after(act, q)

            def stats_half(p, turn, place, bank):
                if bank == 0:
                    scale_rows(p, p, place, turn * 16 + 16)
                    act.wait_ge(sq_step.sem, p * 3 + sq_step.ring)
                    hT_step.done(nc.scalar.copy(hT[:, :, :], pT[:, :, :]))

            def bn():
                act.wait_ge(var_ready, 1)
                nc.scalar.activation(std[:, :], std[:, :], ACT.Sqrt).then_inc(std_ready, 1)
                act.wait_ge(sq_step.sem, NPAIR * 3 + sq_step.ring)
                act.wait_ge(bn_ready, 1)

            def mix_half(p, turn, place, h):
                if h == 0:
                    scale_rows(p, p + MIX, 1 - place, turn * 16 + 16 * ((NPAIR + 1 - (1 - place)) // 2 + 1))
                    act.wait_ge(q_step.sem, p * 3 + q_step.ring)
                    hT_step.done(nc.scalar.copy(hT[:, :, :], pT[:, :, :]))
                if h == 1:
                    act.wait_ge(c_step.sem, p * 2 + c_step.ring)
                    for c in range(3):
                        q_step.after(act, p, c)
                        for m in (2 * c, 2 * c + 1):
                            last = nc.scalar.activation(uT[:, m, :], R[:, 1 + (c + place) % 2, m % 2, :], ACT.Relu,
                                                        bias=b.bn_b[:, m:m + 1], scale=b.bn_a[:, m:m + 1])
                        u_step.done(last)
                if h in (2, 3):
                    j = h - 2
                    if j == 0:
                        ch.restart()
                        act.wait_ge(fs_step.sem, p * 2 + fs_step.ring)
                    c_step.after(act, p, j)
                    o_step.free(act, p, j)
                    ch.do(nc.scalar.activation(squares[:, :], pc[:, 0:CH], ACT.Square, accum_out=nsq[:, j, 0:1]))
                    ch.do(nc.scalar.activation(squares[:, :], pc[:, CH:2 * CH], ACT.Square, accum_out=nsq[:, j, 1:2]))
                    nc.scalar.activation(nrm[:, j, 0:1], nsq[:, j, 0:1], ACT.Sqrt)
                    nc.scalar.activation(nrm[:, j, 1:2], nsq[:, j, 1:2], ACT.Sqrt, bias=nsq[:, j, 0:1])
                    cs_step.done(nc.scalar.copy(cat[:, j, :], pc))
                if h in (4, 5):
                    j = h - 4
                    o_step.after(act, p, j)
                    ch.do(nc.scalar.activation(squares[:, 0:HID], o[:, j, :], ACT.Square, accum_out=osq[:, j:j + 1]))
                    ft_step.free(act, p, j)
                    on_step.done(nc.scalar.activation(onrm[:, j:j + 1], osq[:, j:j + 1], ACT.Sqrt))
                    ot_step.after(act, p, j)
                    f_step.free(act, p, j)
                    oT_step.done(nc.scalar.copy(oT[:, :, :], po))
                if h == 5:
                    for j in range(2):
                        ft_step.after(act, p, j)
                        fs_step.done(nc.scalar.activation(squares[:, 0:D], ft[:, j], ACT.Square,
                                                          accum_out=b.ft_sq[:, bass.ds(p * 2 + j, 1)]))
                        if j == 0:
                            fs_step.after(act, p, 0)

            def dense_job(p):
                dt_step.after(act, p)
                act.dma_start(xg[:, :, :], pairs(b.xn_d, p + 1)).then_inc(xg_in, 16)
                in_step.done(nc.scalar.copy(inT[:, :, :], dT))
                for c in range(2):
                    h_step.after(act, p, c)
                    for m in (2 * c, 2 * c + 1):
                        last = nc.scalar.activation(gT[:, m, :], dh[:, m, :], ACT.Relu, bias=b.b1[:, m:m + 1])
                    gT_step.done(last)
                out_step.after(act, p, 1)
                act.dma_start(pairs(b.y_d, p), ys[:, :, :]).then_inc(yz_out, 16)
                act.dma_start(pairs(b.z_d, p), zs[:, :, :]).then_inc(yz_out, 16)

            schedule(act, lambda it, n, bank: items.act_half(act, it, n, bank), stats_half, bn, mix_half, dense_job)
            items.act_rounds(act)
            ready_pairs(act, b, S_TURNS + M_TURNS, None, dense_job)
            act.wait_ge(yz_out, 32 * (NPAIR + 1))
            act.wait_ge(xg_in, 16 * (NPAIR + 1))

        @block.vector
        def _(dve):
            ch = Chain(dve, chain_v)
            nc.vector.memset(pw[:, :, :], 0.0).then_inc(pw_zero, 1)
            nc.vector.memset(ys[:, :, :], 0.0)
            nc.vector.memset(zs[:, :, :], 0.0).then_inc(yz_open, 1)
            items.dve_start(dve)
            for s in (st_step, o_step, ft_step, ag_step, out_step):
                s.start(dve)
            dve.wait_ge(weights_in, 16 * 11)
            for m in range(6):
                last = nc.vector.tensor_scalar(pw[:, m, :], pw[:, m, :], dw[:, m:m + 1], None, ALU.mult)
            last.then_inc(pw_zero, 1)

            def stats_half(p, turn, place, bank):
                if bank == 1:
                    for c in range(3):
                        sq_step.after(dve, p, c)
                        for m in (2 * c, 2 * c + 1):
                            cols = N - (NPAIR - 1) * 2 * P if isinstance(p, int) and p == NPAIR - 1 else 2 * P
                            last = nc.vector.bn_stats(flat(stats[:, m, bass.ds(p, 1), :]), R[:, 1 + c, m % 2, 0:cols])
                        st_step.done(last)

            def bn():
                ch.restart()
                st_step.after(dve, NPAIR - 1, 2)
                for m in range(6):
                    last = nc.vector.bn_aggr(mv[:, m, :], flat(stats[:, m]))
                ch.do(last)
                nc.vector.tensor_scalar(std[:, :], mv[:, :, 1], 1e-5, None, ALU.add).then_inc(var_ready, 1)
                dve.wait_ge(std_ready, 1)
                ch.do(nc.vector.reciprocal(std[:, :], std[:, :]))
                ch.do(nc.vector.tensor_tensor(b.bn_a[:, :], b.bn_a[:, :], std[:, :], ALU.mult))
                ch.do(nc.vector.tensor_tensor(std[:, :], mv[:, :, 0], b.bn_a[:, :], ALU.mult))
                nc.vector.tensor_tensor(b.bn_b[:, :], b.bn_b[:, :], std[:, :], ALU.subtract).then_inc(bn_ready, 1)

            def factor(out_ap, n_ap, t):
                ch.do(nc.vector.tensor_scalar(t, n_ap, LOG_EPS, None, ALU.max))
                ch.do(nc.vector.reciprocal(t, t))
                ch.do(nc.vector.tensor_scalar(out_ap, n_ap, ATANH_MAX, t, ALU.min, ALU.mult))

            def mix_half(p, turn, place, h):
                if h == 2:
                    ch.restart()
                if h in (3, 4):
                    j = h - 3
                    cs_step.after(dve, p, j)
                    factor(sc[:, 1:2], nrm[:, j, 0:1], sc[:, 0:1])
                    ch.do(nc.vector.tensor_tensor(sc[:, 2:3], sc[:, 1:2], nrm[:, j, 1:2], ALU.mult))
                    factor(sc[:, 4:5], sc[:, 2:3], sc[:, 3:4])
                    ch.do(nc.vector.tensor_tensor(al[:, 0:1], sc[:, 1:2], sc[:, 4:5], ALU.mult))
                    ch.do(nc.vector.tensor_tensor(al[:, 1:2], al[:, 0:1], al[:, 0:1], ALU.mult))
                    q, k, val = (cat[:, j, :].rearrange("p (g c e) -> p c g e", c=3, e=32)[:, c] for c in range(3))
                    ch.do(nc.vector.tensor_scalar(kr[:, :, :], k, 0.0, None, ALU.max))
                    nc.vector.tensor_reduce(out=ks[:, :], in_=kr[:, :, :], op=ALU.add, axis=AX.X)
                    ch.do(nc.vector.tensor_scalar(rv[:, :, :], val, al[:, 0:1], LOG_EPS, ALU.mult, ALU.add))
                    ch.do(nc.vector.reciprocal(rv[:, :, :], rv[:, :, :]))
                    nc.vector.scalar_tensor_tensor(out=rv[:, :, :], in0=val, scalar=al[:, 0:1], in1=rv[:, :, :],
                                                   op0=ALU.mult, op1=ALU.mult)
                    ch.do(nc.vector.scalar_tensor_tensor(
                        out=kr[:, :, :], in0=q, scalar=0.0,
                        in1=ks[:, :].rearrange("p (g o) -> p g o", o=1).to_broadcast([P, G, 32]),
                        op0=ALU.max, op1=ALU.mult))
                    on_step.free(dve, p, j)
                    ot_step.free(dve, p, j)
                    o_step.done(nc.vector.scalar_tensor_tensor(
                        out=o[:, j, :].rearrange("p (g e) -> p g e", e=32), in0=kr[:, :, :], scalar=al[:, 1:2],
                        in1=rv[:, :, :], op0=ALU.mult, op1=ALU.mult))
                if h == 5:
                    fs_step.free(dve, p, 1)
                    stored.free(dve, p)
                    for j in range(2):
                        on_step.after(dve, p, j)
                        factor(sc[:, 6:7], onrm[:, j:j + 1], sc[:, 5:6])
                        f_step.after(dve, p, j)
                        ft_step.done(nc.vector.scalar_tensor_tensor(out=ft[:, j], in0=pf, scalar=sc[:, 6:7],
                                                                    in1=b.bres_bc[:, :], op0=ALU.mult, op1=ALU.add))
                        ft_step.after(dve, p, j)

            def dense_job(p):
                ch.restart()
                rd = b.rdeg[:, bass.ds(p * 2, 2)]
                ch.do(nc.vector.tensor_scalar(rd, b.acc[:, bass.ds(p * 2, 2), D:D + 1].rearrange("p a o -> p (a o)"),
                                              1.0, None, ALU.max))
                ch.do(nc.vector.reciprocal(rd, rd))
                dt_step.free(dve, p)
                for j in range(2):
                    last = nc.vector.tensor_scalar(ag[:, j], flat(b.acc[:, bass.ds(p * 2 + j, 1), 0:D]),
                                                   b.rdeg[:, bass.ds(p * 2 + j, 1)], None, ALU.mult)
                ag_step.done(last)
                dve.wait_ge(yz_out, p * 32 + 32)
                for j in range(2):
                    y_step.after(dve, p, j)
                    nc.vector.tensor_copy(ys[:, j], dy[:, j, 0])
                    out_step.done(nc.vector.tensor_tensor(zs[:, j], dy[:, j, 1], b.b2_bc[:, :], ALU.add))

            schedule(dve, lambda it, n, bank: items.dve_half(dve, it, n, bank), stats_half, bn, mix_half, dense_job)
            items.dve_rounds(dve)
            ready_pairs(dve, b, S_TURNS + M_TURNS, None, dense_job)


def aggregate(nc, name, table_d, b, with_degree):
    with ExitStack() as ctx:
        items = Items(nc, ctx, name, table_d, b, with_degree)
        block = ctx.enter_context(nc.Block())

        @block.gpsimd
        def _(pool):
            items.pool_rounds(pool)

        @block.scalar
        def _(act):
            items.act_start(act)
            with act.Fori(0, ITER) as it:
                for bank in range(2):
                    items.act_half(act, it, it, bank)
            items.act_rounds(act)

        @block.vector
        def _(dve):
            items.dve_start(dve)
            with dve.Fori(0, ITER) as it:
                for bank in range(2):
                    items.dve_half(dve, it, it, bank)
            items.dve_rounds(dve)

        @block.tensor
        def _(pe):
            items.pe_start(pe)
            with pe.Fori(0, ITER) as it:
                for bank in range(2):
                    items.pe_half(pe, it, it, bank)
            items.pe_rounds(pe)


def finish(nc, a, b, out):
    ident, X = b.ident, b.X
    outer = ExitStack()
    with outer:
        def keep(name, shape, dt=F32):
            return outer.enter_context(nc.sbuf_tensor(name, shape, dt))

        moe_w1 = keep("moe_w1", [P, NE, 2, D])
        moe_w2 = keep("moe_w2", [P, NE, 2, D])
        TT = keep("TT", [P, 2, NROWS])
        weight = keep("weight", [P, NT2, NE])
        moe_in = outer.enter_context(nc.semaphore("moe_in"))

        with ExitStack() as ctx:
            def sb(name, shape, dt=F32):
                return ctx.enter_context(nc.sbuf_tensor(name, shape, dt))

            sem = Sems(ctx, nc, "to")
            xr = sb("to_xr", [P, 2, 2, D])
            zr = sb("to_zr", [P, 2, 2, D])
            fr = sb("to_fr", [P, 2, 2, D])
            x1 = sb("to_x1", [P, 2, D])
            ts = sb("to_ts", [P, 2, D])
            tT = sb("to_tT", [P, 2, 2 * P])
            stats = sb("to_stats", [P, 2, 6])
            mv = sb("to_mv", [P, 2, 2])
            std = sb("to_std", [P, 2])
            f_n = sb("to_f_n", [P, NT2])
            f_t = sb("to_f_t", [P, NT2])
            pT = ctx.enter_context(nc.psum_tensor("to_pT", [P, 2, 2 * P], F32))
            pl = ctx.enter_context(nc.psum_tensor("to_pl", [P, 2, NE], F32))
            rows_in = [sem("rows_in0"), sem("rows_in1")]
            chain, fn_ready, ft_ready, softmax_in, exp_ready = (sem("chain"), sem("fn_ready"), sem("ft_ready"),
                                                                sem("softmax_in"), sem("exp_ready"))
            used_step = Step(sem("used"), 2)
            var_step = Step(sem("var"), 1)
            std_step = Step(sem("std"), 1)
            ts_step = Step(sem("ts"), 1)
            tr_step = Step(sem("tr"), 1)
            tT_step = Step(sem("tT"), 1)
            l_step = Step(sem("l"), 1)
            lo_step = Step(sem("lo"), 1)
            block = ctx.enter_context(nc.Block())

            @block.sync
            def _(sp):
                def load(p, turn, place, place_used=True):
                    if place_used:
                        used_step.free(sp, p)
                    for dst, src in ((xr, b.xp_d), (zr, b.z_d), (fr, b.ft_d)):
                        sp.dma_start(dst[:, place], pairs(src, p)).then_inc(rows_in[place], 16)
                load(0, 0, 0, place_used=False)
                load(1, 0, 1, place_used=False)
                for e in range(NE):
                    sp.dma_start(moe_w1[:, e], a["ew1"][e].rearrange("(k p) n -> p k n", p=P)).then_inc(moe_in, 16)
                    sp.dma_start(moe_w2[:, e], a["ew2"][e].rearrange("(k p) n -> p k n", p=P)).then_inc(moe_in, 16)
                with sp.Fori(1, NPAIR // 2) as i:
                    load(i * 2, i, 0)
                    load(i * 2 + 1, i, 1)
                load(NPAIR - 1, NPAIR // 2, 0)

            @block.scalar
            def _(act):
                nc.scalar.activation(f_n[:, :], b.ft_sq[:, :], ACT.Sqrt).then_inc(fn_ready, 1)
                act.wait_ge(fn_ready, 1)
                nc.scalar.activation(f_t[:, :], f_n[:, :], ACT.Tanh).then_inc(ft_ready, 1)
                std_step.start(act)
                tT_step.start(act)

                def body(p, turn, place):
                    var_step.after(act, p)
                    std_step.done(nc.scalar.activation(std[:, :], std[:, :], ACT.Sqrt))
                    tr_step.after(act, p)
                    l_step.free(act, p)
                    lo_step.free(act, p)
                    tT_step.done(nc.scalar.copy(tT[:, :, :], pT[:, :, :]))
                over_pairs(act, body)
                act.wait_ge(softmax_in, 1)
                nc.scalar.activation(weight[:, :, :], weight[:, :, :], ACT.Exp).then_inc(exp_ready, 1)

            @block.tensor
            def _(pe):
                tr_step.start(pe)
                l_step.start(pe)

                def body(p, turn, place):
                    ts_step.after(pe, p)
                    tT_step.free(pe, p)
                    for k in range(2):
                        for j in range(2):
                            last = nc.tensor.transpose(pT[:, k, j * P:(j + 1) * P], ts[:, j, k * P:(k + 1) * P], ident[:, :])
                    tr_step.done(last)
                    tT_step.after(pe, p)
                    lo_step.free(pe, p)
                    for j in range(2):
                        for k in range(2):
                            last = nc.tensor.matmul(pl[:, j, :], tT[:, k, j * P:(j + 1) * P], b.router[:, k, :],
                                                    start=(k == 0), stop=(k == 1))
                    l_step.done(last)
                over_pairs(pe, body)

            @block.vector
            def _(dve):
                ch = Chain(dve, chain)
                for s in (used_step, var_step, ts_step, lo_step):
                    s.start(dve)
                dve.wait_ge(ft_ready, 1)
                ch.do(nc.vector.tensor_scalar(f_n[:, :], f_n[:, :], LOG_EPS, None, ALU.max))
                ch.do(nc.vector.reciprocal(f_n[:, :], f_n[:, :]))
                ch.do(nc.vector.scalar_tensor_tensor(out=f_t[:, :], in0=f_t[:, :], scalar=MAXNORM, in1=f_n[:, :],
                                                     op0=ALU.min, op1=ALU.mult))

                def body(p, turn, place):
                    ch.restart()
                    lo_step.free(dve, p)
                    dve.wait_ge(rows_in[place], turn * 48 + 48)
                    ch.do(nc.vector.tensor_tensor(x1[:, :, :], xr[:, place], zr[:, place], ALU.add))
                    for j in range(2):
                        last = nc.vector.scalar_tensor_tensor(
                            out=x1[:, j], in0=fr[:, place, j], scalar=f_t[:, bass.ds(p * 2 + j, 1)], in1=x1[:, j],
                            op0=ALU.mult, op1=ALU.add)
                    used_step.done(last)
                    used_step.after(dve, p)
                    for j in range(2):
                        last = nc.vector.scalar_tensor_tensor(
                            out=x1[:, j], in0=flat(b.acc[:, bass.ds(p * 2 + j, 1), 0:D]),
                            scalar=b.rdeg[:, bass.ds(p * 2 + j, 1)], in1=x1[:, j], op0=ALU.mult, op1=ALU.add)
                    ch.do(last)
                    for j in range(2):
                        last = nc.vector.bn_stats(stats[:, j, :], x1[:, j])
                    ch.do(last)
                    for j in range(2):
                        last = nc.vector.bn_aggr(mv[:, j, :], stats[:, j, :])
                    ch.do(last)
                    var_step.done(nc.vector.tensor_scalar(std[:, :], mv[:, :, 1], LN_EPS, None, ALU.add))
                    std_step.after(dve, p)
                    ch.do(nc.vector.reciprocal(std[:, :], std[:, :]))
                    tr_step.free(dve, p)
                    for j in range(2):
                        last = nc.vector.tensor_scalar(ts[:, j], x1[:, j], mv[:, j, 0:1], std[:, j:j + 1],
                                                       ALU.subtract, ALU.mult)
                    ts_step.done(last)
                    ts_step.after(dve, p)
                    nc.vector.tensor_tensor(X[:, bass.ds(p * 2, 2), :], x1[:, :, :], ts[:, :, :], ALU.add)
                    tT_step.after(dve, p)
                    nc.vector.tensor_copy(TT[:, :, bass.ds(p * 2 * P, 2 * P)], tT[:, :, :])
                    l_step.after(dve, p)
                    lo_step.done(nc.vector.tensor_copy(weight[:, bass.ds(p * 2, 2), :], pl[:, :, :]))
                over_pairs(dve, body)
                lo_step.after(dve, NPAIR - 1)
                ch.restart()
                w = weight[:, :, :]
                big = fr[:, :, :, :].rearrange("p a b c -> p (a b c)")
                tmp = [big[:, i * NT2 * NE:(i + 1) * NT2 * NE].rearrange("p (t e) -> p t e", e=NE) for i in range(2)]
                big2 = zr[:, :, :, :].rearrange("p a b c -> p (a b c)")
                rank, picked = (big2[:, i * NT2 * NE:(i + 1) * NT2 * NE].rearrange("p (t e) -> p t e", e=NE)
                                for i in range(2))
                red = f_n[:, :]

                def wide(ap):
                    return ap.rearrange("p (t o) -> p t o", o=1).to_broadcast([P, NT2, NE])

                for e in range(NE):
                    last = nc.vector.memset(rank[:, :, e], float(NE - e))
                ch.do(last)
                ch.do(nc.vector.tensor_reduce(out=red, in_=w, op=ALU.max, axis=AX.X))
                nc.vector.tensor_tensor(w, w, wide(red), ALU.subtract).then_inc(softmax_in, 1)
                dve.wait_ge(exp_ready, 1)
                ch.do(nc.vector.tensor_reduce(out=red, in_=w, op=ALU.add, axis=AX.X))
                ch.do(nc.vector.reciprocal(red, red))
                ch.do(nc.vector.tensor_tensor(w, w, wide(red), ALU.mult))
                ch.do(nc.vector.tensor_copy(tmp[0], w))
                for turn in range(2):
                    ch.do(nc.vector.tensor_reduce(out=red, in_=tmp[0], op=ALU.max, axis=AX.X))
                    ch.do(nc.vector.tensor_tensor(tmp[1], tmp[0], wide(red), ALU.is_equal))
                    ch.do(nc.vector.tensor_tensor(tmp[1], tmp[1], rank, ALU.mult))
                    ch.do(nc.vector.tensor_reduce(out=red, in_=tmp[1], op=ALU.max, axis=AX.X))
                    ch.do(nc.vector.tensor_tensor(tmp[1], rank, wide(red), ALU.is_equal))
                    if turn == 0:
                        ch.do(nc.vector.tensor_copy(picked, tmp[1]))
                        ch.do(nc.vector.scalar_tensor_tensor(out=tmp[0], in0=tmp[1], scalar=-2.0, in1=tmp[0],
                                                             op0=ALU.mult, op1=ALU.add))
                    else:
                        ch.do(nc.vector.tensor_tensor(picked, picked, tmp[1], ALU.add))
                ch.do(nc.vector.tensor_tensor(w, w, picked, ALU.mult))
                ch.do(nc.vector.tensor_reduce(out=red, in_=w, op=ALU.add, axis=AX.X))
                ch.do(nc.vector.tensor_scalar(red, red, 1e-12, None, ALU.max))
                ch.do(nc.vector.reciprocal(red, red))
                ch.do(nc.vector.tensor_tensor(w, w, wide(red), ALU.mult))

        with ExitStack() as ctx:
            def sb(name, shape, dt=F32):
                return ctx.enter_context(nc.sbuf_tensor(name, shape, dt))

            sem = Sems(ctx, nc, "ex")
            gT = sb("ex_gT", [P, 2, 2, 2 * P])
            cs = sb("ex_cs", [P, 2, 2, NE])
            cT = sb("ex_cT", [NE, 2 * P])
            ph = ctx.enter_context(nc.psum_tensor("ex_ph", [P, 2, 2, 2 * P], F32))
            py = ctx.enter_context(nc.psum_tensor("ex_py", [P, 2, 2, D], F32))
            pc = ctx.enter_context(nc.psum_tensor("ex_pc", [P, 512], F32))
            pb = ctx.enter_context(nc.psum_tensor("ex_pb", [P, 2, D], F32))
            out_done, chain = sem("out_done"), sem("chain")
            h_step = Step(sem("h"), 2, NE)
            g_step = Step(sem("g"), 2, NE)
            y_step = Step(sem("y"), 2, NE)
            add_step = Step(sem("add"), 2, NE)
            cs_step = Step(sem("cs"), 2)
            ct_step = Step(sem("ct"), 1)
            cT_step = Step(sem("cT"), 1)
            bias_step = Step(sem("bias"), 1)
            fin_step = Step(sem("fin"), 1)
            block = ctx.enter_context(nc.Block())

            @block.sync
            def _(sp):
                def store(p, turn, place):
                    fin_step.after(sp, p)
                    sp.dma_start(pairs(out, p), X[:, bass.ds(p * 2, 2), :]).then_inc(out_done, 16)
                with sp.Fori(0, NPAIR - 1) as p:
                    store(p, 0, 0)
                fin_step.after(sp, NPAIR - 1)
                sp.dma_start(out[(NT - 1) * P:N, :], X[0:LAST, NT - 1, :]).then_inc(out_done, 16)
                sp.wait_ge(out_done, 16 * NPAIR)

            @block.tensor
            def _(pe):
                for s in (h_step, y_step, ct_step, bias_step):
                    s.start(pe)
                pe.wait_ge(moe_in, 16 * 2 * NE)

                def first(p, e):
                    g_step.free(pe, p, e)
                    for m in range(2):
                        for k in range(2):
                            last = nc.tensor.matmul(ph[:, e % 2, m], moe_w1[:, e, k, m * P:(m + 1) * P],
                                                    TT[:, k, bass.ds(p * 2 * P, 2 * P)], start=(k == 0), stop=(k == 1))
                    h_step.done(last)

                def second(p, e):
                    g_step.after(pe, p, e)
                    add_step.free(pe, p, e)
                    for j in range(2):
                        for k in range(2):
                            last = nc.tensor.matmul(py[:, e % 2, j], gT[:, e % 2, k, j * P:(j + 1) * P], moe_w2[:, e, k, :],
                                                    start=(k == 0), stop=(k == 1))
                    y_step.done(last)

                def body(p, turn, place, last_pair=False):
                    cs_step.after(pe, p)
                    cT_step.free(pe, p)
                    for j in range(2):
                        last = nc.tensor.transpose(pc[0:NE, j * P:(j + 1) * P], cs[:, place, j, :], ident[:, :])
                    ct_step.done(last)
                    for e in range(NE):
                        if e + 1 < NE:
                            first(p, e + 1)
                        elif not last_pair:
                            first(p + 1, 0)
                        second(p, e)
                    cT_step.after(pe, p)
                    fin_step.free(pe, p)
                    for j in range(2):
                        last = nc.tensor.matmul(pb[:, j], cT[0:NE, j * P:(j + 1) * P], b.moe_b2[:, :], start=True, stop=True)
                    bias_step.done(last)

                first(0, 0)
                with pe.Fori(0, NPAIR // 2) as i:
                    body(i * 2, i, 0)
                    body(i * 2 + 1, i, 1)
                body(NPAIR - 1, NPAIR // 2, 0, last_pair=True)

            @block.scalar
            def _(act):
                g_step.start(act)
                cT_step.start(act)

                def body(p, turn, place):
                    for e in range(NE):
                        h_step.after(act, p, e)
                        y_step.free(act, p, e)
                        for m in range(2):
                            last = nc.scalar.activation(gT[:, e % 2, m, :], ph[:, e % 2, m], ACT.Gelu,
                                                        bias=b.moe_b1[:, e, m:m + 1])
                        g_step.done(last)
                        if e == 3:
                            ct_step.after(act, p)
                            bias_step.free(act, p)
                            cT_step.done(nc.scalar.copy(cT[:, :], pc[0:NE, 0:2 * P]))
                over_pairs(act, body)

            @block.vector
            def _(dve):
                add_step.start(dve)
                cs_step.start(dve)
                fin_step.start(dve)

                def stage(p, turn, place):
                    dve.wait_ge(ct_step.sem, p)
                    cs_step.done(nc.vector.tensor_copy(cs[:, place], weight[:, bass.ds(p * 2, 2), :]))

                def body(p, turn, place, last_pair=False):
                    for e in range(NE):
                        y_step.after(dve, p, e)
                        dve.wait_ge(add_step.sem, p * NE + e + add_step.ring)
                        for j in range(2):
                            at = flat(X[:, bass.ds(p * 2 + j, 1), :])
                            last = nc.vector.scalar_tensor_tensor(
                                out=at, in0=py[:, e % 2, j], scalar=flat(weight[:, bass.ds(p * 2 + j, 1), e:e + 1]),
                                in1=at, op0=ALU.mult, op1=ALU.add)
                        add_step.done(last)
                    if not last_pair:
                        stage(p + 1, turn + place, 1 - place)
                    bias_step.after(dve, p)
                    add_step.after(dve, p, NE - 1)
                    at = X[:, bass.ds(p * 2, 2), :]
                    fin_step.done(nc.vector.tensor_tensor(at, at, pb[:, :, :], ALU.add))
                cs_step.done(nc.vector.tensor_copy(cs[:, 0], weight[:, 0:2, :]))
                with dve.Fori(0, NPAIR // 2) as i:
                    body(i * 2, i, 0)
                    body(i * 2 + 1, i, 1)
                body(NPAIR - 1, NPAIR // 2, 0, last_pair=True)


def kernel(**inputs):
    import numpy as np
    import concourse.bacc as bacc
    from concourse.bass_utils import run_bass_kernel_spmd

    laid_out = {
        "x": inputs["x"], "src": inputs["src"], "dst": inputs["dst"],
        "W1l": inputs["L0_gnn_W1l"], "b1": inputs["L0_gnn_b1"], "W1r": inputs["L0_gnn_W1r"],
        "W2l": inputs["L0_gnn_W2l"], "b2": inputs["L0_gnn_b2"], "W2r": inputs["L0_gnn_W2r"],
        "w_qkv": np.transpose(inputs["L0_mix_w_qkv"], (2, 1, 0)),
        "gamma": inputs["L0_mix_bn_gamma"], "beta": inputs["L0_mix_bn_beta"],
        "w_dw": np.transpose(inputs["L0_mix_w_dw"], (2, 1, 0)),
        "w_pw": np.transpose(np.reshape(inputs["L0_mix_w_pw"], (CH // 32, 32, 32)), (0, 2, 1)),
        "w_res": np.transpose(np.reshape(inputs["L0_mix_w_res"], (D, HID)), (1, 0)),
        "b_res": inputs["L0_mix_b_res"], "routerT": np.transpose(inputs["L0_ffn_router_w"], (1, 0)),
        "ew1": inputs["L0_ffn_w1"], "eb1": inputs["L0_ffn_b1"], "ew2": inputs["L0_ffn_w2"], "eb2": inputs["L0_ffn_b2"],
    }
    nc = bacc.Bacc("TRN2", target_bir_lowering=False, num_devices=1)
    arrays, a = {}, {}
    for name, value in laid_out.items():
        value = np.ascontiguousarray(value)
        arrays[f"in_{name}"] = value
        a[name] = nc.dram_tensor(f"in_{name}", value.shape, mybir.dt.from_np(value.dtype), kind="ExternalInput").ap()
    out = nc.dram_tensor("out_0", (N, D), F32, kind="ExternalOutput").ap()
    gnn_mix_moe(nc, a, out)
    r = run_bass_kernel_spmd(nc, [arrays], core_ids=[0])
    return r.results[0]["out_0"]
```
